# Optimizing a Trainium2 kernel written in Bass

```python
import numpy as np
import jax
import jax.numpy as jnp

def _softmax(x, axis=-1):
    return jax.nn.softmax(x, axis=axis)

def _gelu(x):
    return jax.nn.gelu(x, approximate=True)

def _silu(x):
    return jax.nn.silu(x)

def _sigmoid(x):
    return jax.nn.sigmoid(x)

def _layernorm(x, axis=-1, eps=1e-05):
    m = jnp.mean(x, axis=axis, keepdims=True)
    v = jnp.var(x, axis=axis, keepdims=True)
    return (x - m) / jnp.sqrt(v + eps)

def _scatter_add(tgt, idx, src, axis=0):
    return tgt.at[idx].add(src)

def _segment_sum(src, seg, n):
    return jax.ops.segment_sum(src, seg, n)
kernel_name = 'mk_gnn_resnorm_d4_gnn_r8_301b61'

def setup_inputs(seed: int=0):
    np.random.seed(seed)
    _w = jnp.asarray

    def _rec_inputs():
        import jax
        import jax.numpy as jnp
        _gk = jax.random.key(seed)
        x = -0.0003713 + 1 * jax.random.normal(jax.random.fold_in(_gk, 1), (6250, 256), jnp.float32)
        _s = jax.random.randint(jax.random.fold_in(_gk, 2), (50000,), 0, 6250, jnp.int32)
        _d = jax.random.randint(jax.random.fold_in(_gk, 3), (50000,), 0, 6250, jnp.int32)
        _loop = jnp.arange(6250, dtype=jnp.int32)
        src = jnp.concatenate([_s, _d, _loop])
        dst = jnp.concatenate([_d, _s, _loop])
        _o = jnp.argsort(dst, stable=True)
        src = src[_o]
        dst = dst[_o]
        edge_attr_256 = -6.47781e-05 + 0.999943 * jax.random.normal(jax.random.fold_in(_gk, 12), (106250, 256), jnp.float32)
        edge_type_16 = jax.random.randint(jax.random.fold_in(_gk, 13), (106250,), 0, 16, jnp.int32)
        return (x, src, dst, edge_attr_256, edge_type_16)
    x, src, dst, edge_attr_256, edge_type_16 = _rec_inputs()

    def _L0_gnn_setup():
        import jax, jax.numpy as jnp
        import numpy as np
        N_NODES = 6250
        N_EDGES = 100000
        D_IN = 256
        D_OUT = 256
        key = jax.random.key(seed)
        k_feat, k_src, k_dst, k_ws, k_wn, k_b = jax.random.split(key, 6)
        feat = jax.random.normal(k_feat, (N_NODES, D_IN), dtype=jnp.float32)
        src = jax.random.randint(k_src, (N_EDGES,), 0, N_NODES)
        dst = jax.random.randint(k_dst, (N_EDGES,), 0, N_NODES)
        scale = 1.0 / np.sqrt(D_IN)
        W_self = jax.random.normal(k_ws, (D_IN, D_OUT), dtype=jnp.float32) * scale
        W_neigh = jax.random.normal(k_wn, (D_IN, D_OUT), dtype=jnp.float32) * scale
        b = jnp.zeros((D_OUT,), dtype=jnp.float32)
        return {'feat': feat, 'W_self': W_self, 'W_neigh': W_neigh, 'b': b, 'src': src, 'dst': dst}
    _L0_gnn_all = _L0_gnn_setup()
    _L0_gnn_in = {k: v for k, v in _L0_gnn_all.items() if k in ('W_self', 'W_neigh', 'b')}
    del _L0_gnn_all

    def _L1_gnn_setup():
        import jax, jax.numpy as jnp
        import numpy as np
        N_NODES = 6250
        N_EDGES = 100000
        HDIM = 256
        NUMRELS = 16

        def _gru_cell(x, h, w_ih, w_hh, b_ih, b_hh):
            gi = x @ w_ih.T + b_ih
            gh = h @ w_hh.T + b_hh
            i_r, i_z, i_n = jnp.split(gi, 3, axis=-1)
            h_r, h_z, h_n = jnp.split(gh, 3, axis=-1)
            r = jax.nn.sigmoid(i_r + h_r)
            z = jax.nn.sigmoid(i_z + h_z)
            n = jnp.tanh(i_n + r * h_n)
            return (1.0 - z) * n + z * h
        key = jax.random.key(seed)
        ks = jax.random.split(key, 9)
        h = jax.random.normal(ks[0], (N_NODES, HDIM), dtype=jnp.float32)
        relvectors = jax.random.normal(ks[1], (NUMRELS, HDIM), dtype=jnp.float32)
        s = 1.0 / np.sqrt(HDIM)
        w_ih = jax.random.uniform(ks[2], (3 * HDIM, HDIM), minval=-s, maxval=s, dtype=jnp.float32)
        w_hh = jax.random.uniform(ks[3], (3 * HDIM, HDIM), minval=-s, maxval=s, dtype=jnp.float32)
        b_ih = jax.random.uniform(ks[4], (3 * HDIM,), minval=-s, maxval=s, dtype=jnp.float32)
        b_hh = jax.random.uniform(ks[5], (3 * HDIM,), minval=-s, maxval=s, dtype=jnp.float32)
        edge_src = jax.random.randint(ks[6], (N_EDGES,), 0, N_NODES, dtype=jnp.int32)
        edge_dst = jax.random.randint(ks[7], (N_EDGES,), 0, N_NODES, dtype=jnp.int32)
        edge_rel = jax.random.randint(ks[8], (N_EDGES,), 0, NUMRELS, dtype=jnp.int32)
        return {'h': h, 'relvectors': relvectors, 'w_ih': w_ih, 'w_hh': w_hh, 'b_ih': b_ih, 'b_hh': b_hh, 'edge_src': edge_src, 'edge_dst': edge_dst, 'edge_rel': edge_rel}
    _L1_gnn_all = _L1_gnn_setup()
    _L1_gnn_in = {k: v for k, v in _L1_gnn_all.items() if k in ('relvectors', 'w_ih', 'w_hh', 'b_ih', 'b_hh')}
    del _L1_gnn_all

    def _L2_gnn_setup():
        import jax, jax.numpy as jnp
        import numpy as np
        N_NODES = 6250
        N_EDGES = 100000
        IN_FEAT = 256
        NUM_HEADS = 8
        HEAD_DIM = 32
        NEG_SLOPE = 0.2
        key = jax.random.key(seed)
        ks = jax.random.split(key, 10)
        node_feat = jax.random.normal(ks[0], (N_NODES, IN_FEAT), dtype=jnp.float32)
        edge_feat = jax.random.normal(ks[1], (N_EDGES, IN_FEAT), dtype=jnp.float32)
        src = jax.random.randint(ks[2], (N_EDGES,), 0, N_NODES, dtype=jnp.int32)
        dst = jax.random.randint(ks[3], (N_EDGES,), 0, N_NODES, dtype=jnp.int32)
        scale = 1.0 / np.sqrt(IN_FEAT)
        W = jax.random.normal(ks[4], (NUM_HEADS * HEAD_DIM, IN_FEAT), dtype=jnp.float32) * scale
        We = jax.random.normal(ks[5], (NUM_HEADS * HEAD_DIM, IN_FEAT), dtype=jnp.float32) * scale
        attn_l = jax.random.normal(ks[6], (NUM_HEADS, HEAD_DIM), dtype=jnp.float32) * scale
        attn_r = jax.random.normal(ks[7], (NUM_HEADS, HEAD_DIM), dtype=jnp.float32) * scale
        attn_e = jax.random.normal(ks[8], (NUM_HEADS, HEAD_DIM), dtype=jnp.float32) * scale
        bias = jnp.zeros((NUM_HEADS * HEAD_DIM,), dtype=jnp.float32)
        return {'node_feat': node_feat, 'edge_feat': edge_feat, 'src': src, 'dst': dst, 'W': W, 'We': We, 'attn_l': attn_l, 'attn_r': attn_r, 'attn_e': attn_e, 'bias': bias}
    _L2_gnn_all = _L2_gnn_setup()
    _L2_gnn_in = {k: v for k, v in _L2_gnn_all.items() if k in ('W', 'We', 'attn_l', 'attn_r', 'attn_e', 'bias')}
    del _L2_gnn_all

    def _L3_gnn_setup():
        import jax, jax.numpy as jnp
        import numpy as np
        NEG_SLOPE = 0.2
        N_NODES = 6250
        N_EDGES = 100000
        IN_DIM = 256
        HID_DIM = 256
        HEADS = 8
        HEAD_DIM = HID_DIM // HEADS

        def gat_layer(x, src, dst, W, al, ar, b):
            N = x.shape[0]
            feat = (x @ W).reshape(N, HEADS, HEAD_DIM)
            el = jnp.sum(feat * al[None], axis=-1)
            er = jnp.sum(feat * ar[None], axis=-1)
            e = el[src] + er[dst]
            e = jnp.where(e > 0, e, NEG_SLOPE * e)
            m = jax.ops.segment_max(e, dst, num_segments=N)
            a = jnp.exp(e - m[dst])
            denom = jax.ops.segment_sum(a, dst, num_segments=N)
            alpha = a / denom[dst]
            msg = feat[src] * alpha[:, :, None]
            out = jax.ops.segment_sum(msg, dst, num_segments=N)
            out = out + b.reshape(1, HEADS, HEAD_DIM)
            out = jax.nn.relu(out)
            return out.reshape(N, HID_DIM)
        key = jax.random.key(seed)
        ks = jax.random.split(key, 12)

        def glorot(k, shape):
            fan = sum(shape[-2:]) if len(shape) > 1 else shape[-1] + 1
            return jax.random.normal(k, shape, jnp.float32) * jnp.sqrt(2.0 / fan)
        return {'data': jax.random.normal(ks[0], (N_NODES, IN_DIM), jnp.float32), 'src': jax.random.randint(ks[1], (N_EDGES,), 0, N_NODES), 'dst': jax.random.randint(ks[2], (N_EDGES,), 0, N_NODES), 'W1': glorot(ks[3], (IN_DIM, HID_DIM)), 'al1': glorot(ks[4], (HEADS, HEAD_DIM)), 'ar1': glorot(ks[5], (HEADS, HEAD_DIM)), 'b1': jnp.zeros((HID_DIM,), jnp.float32), 'W2': glorot(ks[6], (HID_DIM, HID_DIM)), 'al2': glorot(ks[7], (HEADS, HEAD_DIM)), 'ar2': glorot(ks[8], (HEADS, HEAD_DIM)), 'b2': jnp.zeros((HID_DIM,), jnp.float32)}
    _L3_gnn_all = _L3_gnn_setup()
    _L3_gnn_in = {k: v for k, v in _L3_gnn_all.items() if k in ('W1', 'al1', 'ar1', 'b1', 'W2', 'al2', 'ar2', 'b2')}
    del _L3_gnn_all
    return {'x': x, 'src': src, 'dst': dst, 'edge_attr_256': edge_attr_256, 'edge_type_16': edge_type_16, 'L0_gnn_W_self': _L0_gnn_in['W_self'], 'L0_gnn_W_neigh': _L0_gnn_in['W_neigh'], 'L0_gnn_b': _L0_gnn_in['b'], 'L1_gnn_relvectors': _L1_gnn_in['relvectors'], 'L1_gnn_w_ih': _L1_gnn_in['w_ih'], 'L1_gnn_w_hh': _L1_gnn_in['w_hh'], 'L1_gnn_b_ih': _L1_gnn_in['b_ih'], 'L1_gnn_b_hh': _L1_gnn_in['b_hh'], 'L2_gnn_W': _L2_gnn_in['W'], 'L2_gnn_We': _L2_gnn_in['We'], 'L2_gnn_attn_l': _L2_gnn_in['attn_l'], 'L2_gnn_attn_r': _L2_gnn_in['attn_r'], 'L2_gnn_attn_e': _L2_gnn_in['attn_e'], 'L2_gnn_bias': _L2_gnn_in['bias'], 'L3_gnn_W1': _L3_gnn_in['W1'], 'L3_gnn_al1': _L3_gnn_in['al1'], 'L3_gnn_ar1': _L3_gnn_in['ar1'], 'L3_gnn_b1': _L3_gnn_in['b1'], 'L3_gnn_W2': _L3_gnn_in['W2'], 'L3_gnn_al2': _L3_gnn_in['al2'], 'L3_gnn_ar2': _L3_gnn_in['ar2'], 'L3_gnn_b2': _L3_gnn_in['b2']}

def reference(x, src, dst, edge_attr_256, edge_type_16, L0_gnn_W_self, L0_gnn_W_neigh, L0_gnn_b, L1_gnn_relvectors, L1_gnn_w_ih, L1_gnn_w_hh, L1_gnn_b_ih, L1_gnn_b_hh, L2_gnn_W, L2_gnn_We, L2_gnn_attn_l, L2_gnn_attn_r, L2_gnn_attn_e, L2_gnn_bias, L3_gnn_W1, L3_gnn_al1, L3_gnn_ar1, L3_gnn_b1, L3_gnn_W2, L3_gnn_al2, L3_gnn_ar2, L3_gnn_b2):
    import jax
    import jax.numpy as jnp

    def _L0_gnn_ref(feat, W_self, W_neigh, b, src, dst):
        import jax, jax.numpy as jnp
        import numpy as np
        N_NODES = 6250
        N_EDGES = 100000
        D_IN = 256
        D_OUT = 256
        n = feat.shape[0]
        msg = feat[src]
        agg = jax.ops.segment_sum(msg, dst, num_segments=n)
        deg = jax.ops.segment_sum(jnp.ones_like(dst, dtype=feat.dtype), dst, num_segments=n)
        h_neigh = agg / jnp.maximum(deg, 1.0)[:, None]
        out = feat @ W_self + h_neigh @ W_neigh + b
        return out

    def _L1_gnn_ref(h, relvectors, w_ih, w_hh, b_ih, b_hh, edge_src, edge_dst, edge_rel):
        import jax, jax.numpy as jnp
        import numpy as np
        N_NODES = 6250
        N_EDGES = 100000
        HDIM = 256
        NUMRELS = 16

        def _gru_cell(x, h, w_ih, w_hh, b_ih, b_hh):
            gi = x @ w_ih.T + b_ih
            gh = h @ w_hh.T + b_hh
            i_r, i_z, i_n = jnp.split(gi, 3, axis=-1)
            h_r, h_z, h_n = jnp.split(gh, 3, axis=-1)
            r = jax.nn.sigmoid(i_r + h_r)
            z = jax.nn.sigmoid(i_z + h_z)
            n = jnp.tanh(i_n + r * h_n)
            return (1.0 - z) * n + z * h
        msg = h[edge_src] + relvectors[edge_rel]
        red = jax.ops.segment_sum(msg, edge_dst, num_segments=h.shape[0])
        return _gru_cell(red, h, w_ih, w_hh, b_ih, b_hh)

    def _L2_gnn_ref(node_feat, edge_feat, src, dst, W, We, attn_l, attn_r, attn_e, bias):
        import jax, jax.numpy as jnp
        import numpy as np
        N_NODES = 6250
        N_EDGES = 100000
        IN_FEAT = 256
        NUM_HEADS = 8
        HEAD_DIM = 32
        NEG_SLOPE = 0.2
        N = node_feat.shape[0]
        H, D = (NUM_HEADS, HEAD_DIM)
        feat_src = (node_feat @ W.T).reshape(N, H, D)
        feat_e = (edge_feat @ We.T).reshape(-1, H, D)
        el = jnp.einsum('nhd,hd->nh', feat_src, attn_l)
        er = jnp.einsum('nhd,hd->nh', feat_src, attn_r)
        ee = jnp.einsum('ehd,hd->eh', feat_e, attn_e)
        score = jax.nn.leaky_relu(el[src] + er[dst] + ee, NEG_SLOPE)
        smax = jax.ops.segment_max(score, dst, num_segments=N)
        smax = jnp.where(jnp.isfinite(smax), smax, 0.0)
        ex = jnp.exp(score - smax[dst])
        denom = jax.ops.segment_sum(ex, dst, num_segments=N)
        alpha = ex / denom[dst]
        msg = (feat_src[src] + feat_e) * alpha[:, :, None]
        rst = jax.ops.segment_sum(msg, dst, num_segments=N)
        rst = rst + node_feat.reshape(N, H, D) + bias.reshape(1, H, D)
        out = jax.nn.relu(rst)
        return out.reshape(N, H * D)

    def _L3_gnn_ref(data, src, dst, W1, al1, ar1, b1, W2, al2, ar2, b2):
        import jax, jax.numpy as jnp
        import numpy as np
        NEG_SLOPE = 0.2
        N_NODES = 6250
        N_EDGES = 100000
        IN_DIM = 256
        HID_DIM = 256
        HEADS = 8
        HEAD_DIM = HID_DIM // HEADS

        def gat_layer(x, src, dst, W, al, ar, b):
            N = x.shape[0]
            feat = (x @ W).reshape(N, HEADS, HEAD_DIM)
            el = jnp.sum(feat * al[None], axis=-1)
            er = jnp.sum(feat * ar[None], axis=-1)
            e = el[src] + er[dst]
            e = jnp.where(e > 0, e, NEG_SLOPE * e)
            m = jax.ops.segment_max(e, dst, num_segments=N)
            a = jnp.exp(e - m[dst])
            denom = jax.ops.segment_sum(a, dst, num_segments=N)
            alpha = a / denom[dst]
            msg = feat[src] * alpha[:, :, None]
            out = jax.ops.segment_sum(msg, dst, num_segments=N)
            out = out + b.reshape(1, HEADS, HEAD_DIM)
            out = jax.nn.relu(out)
            return out.reshape(N, HID_DIM)
        h = gat_layer(data, src, dst, W1, al1, ar1, b1)
        h = gat_layer(h, src, dst, W2, al2, ar2, b2)
        return h
    x = _layernorm(x + _L0_gnn_ref(x, L0_gnn_W_self, L0_gnn_W_neigh, L0_gnn_b, src, dst), axis=-1)
    x = _layernorm(x + _L1_gnn_ref(x, L1_gnn_relvectors, L1_gnn_w_ih, L1_gnn_w_hh, L1_gnn_b_ih, L1_gnn_b_hh, src, dst, edge_type_16), axis=-1)
    x = _layernorm(x + _L2_gnn_ref(x, edge_attr_256, src, dst, L2_gnn_W, L2_gnn_We, L2_gnn_attn_l, L2_gnn_attn_r, L2_gnn_attn_e, L2_gnn_bias), axis=-1)
    x = _layernorm(x + _L3_gnn_ref(x, src, dst, L3_gnn_W1, L3_gnn_al1, L3_gnn_ar1, L3_gnn_b1, L3_gnn_W2, L3_gnn_al2, L3_gnn_ar2, L3_gnn_b2), axis=-1)
    return x

_drawn_inputs = setup_inputs


def setup_inputs(seed=0):
    import zlib

    import numpy as np

    out = dict(_drawn_inputs(seed))
    spreads = {'L0_gnn_b': (0.0, 0.1),
     'L2_gnn_bias': (0.0, 0.1),
     'L3_gnn_b1': (0.0, 0.1),
     'L3_gnn_b2': (0.0, 0.1)}
    factors = {'L1_gnn_b_ih': 8.0,
     'L1_gnn_b_hh': 8.0,
     'L2_gnn_attn_r': 3.148,
     'L3_gnn_ar1': 5.094,
     'L3_gnn_al2': 7.297,
     'L3_gnn_ar2': 22.192}
    for name, (base, spread) in spreads.items():
        noise = np.random.default_rng([zlib.crc32(name.encode()), seed]).standard_normal(out[name].shape)
        drawn = base * np.exp(spread * noise) if base else spread * noise
        out[name] = jnp.asarray(drawn.astype(out[name].dtype))
    for name, factor in factors.items():
        out[name] = (out[name] * factor).astype(out[name].dtype)
    return out
```

```python
from contextlib import ExitStack

import concourse.bass as bass
from concourse import mybir

F32 = mybir.dt.float32
I32 = mybir.dt.int32
ALU = mybir.AluOpType
ACT = mybir.ActivationFunctionType
ENG = mybir.EngineType

P = 128
N = 6250
E = 106250
D = 256
H = 8
HD = D // H
NREL = 16
BLOCKS = -(-N // P)
TILES = -(-E // P)
G = 8
SLOTS = 3
GROUPS = -(-(TILES + BLOCKS - 1) // (G * SLOTS)) * SLOTS
LOOPS = GROUPS // SLOTS
CHUNKS = -(-(GROUPS + 1) * G // P)
KPAD = CHUNKS * P
GE = G * P
NPAD = BLOCKS * P
TROWS = TILES + 1
HW = HD + 1
FW = H * HW
ROW = FW + H
BATCH = 7
NBATCH = BLOCKS // BATCH
BIG = 1.0e30
EPS = 1e-5
SLOPE = 0.2
assert BLOCKS % BATCH == 0 and (GROUPS + 1) * G <= KPAD


class Count:

    def __init__(self, handle, per, credit):
        self.h, self.per, self.base = handle, per, per * credit

    def at(self, unit, part=None):
        return unit * self.per + (self.base + (self.per if part is None else part))

    def phase_ended(self, units):
        self.base += self.per * units


def build(nc, a):
    ctx = ExitStack()
    with ctx:
        def sb(name, shape, dt=F32):
            return ctx.enter_context(nc.sbuf_tensor(name, shape, dt))

        def sem(name):
            return ctx.enter_context(nc.semaphore(name))

        ps = ctx.enter_context(nc.psum_tensor("ps", [P, 8, 512], F32))

        md_lin = nc.dram_tensor("md_lin", [KPAD * P + 1], F32, kind="Internal").ap()
        rst_dram = nc.dram_tensor("rst_dram", [KPAD * P], F32, kind="Internal").ap()
        x1_dram = nc.dram_tensor("x1_dram", [NPAD, D], F32, kind="Internal").ap()
        x2_dram = nc.dram_tensor("x2_dram", [NPAD, D], F32, kind="Internal").ap()
        x3_dram = nc.dram_tensor("x3_dram", [NPAD, D], F32, kind="Internal").ap()
        tab_dram = [nc.dram_tensor(f"tab{n}_dram", [NPAD, ROW], F32, kind="Internal").ap() for n in range(3)]

        ident = sb("ident", [P, P])
        iota = sb("iota", [P, P])
        ones = sb("ones", [P, P])
        src_t = sb("src_t", [P, KPAD], I32)
        md_t = sb("md_t", [P, KPAD])
        type_t = sb("type_t", [P, KPAD])
        blk_row = sb("blk_row", [1, KPAD], I32)
        tile_row = sb("tile_row", [1, KPAD], I32)
        open_md = sb("open_md", [H, GROUPS + 1])

        acc = sb("acc", [P, BLOCKS, ROW])
        er_sb = sb("er_sb", [P, BLOCKS * H])

        rows = sb("rows", [P, SLOTS, G, ROW])
        idx = sb("idx", [P, SLOTS, G], I32)
        hot = sb("hot", [P, SLOTS, G, P])

        def per_group(name, per):
            return Count(sem(name), per, SLOTS)

        def per_block(name, per=1):
            return Count(sem(name), per, BATCH)

        cleared = Count(sem("cleared"), 2, 0)
        settled = sem("settled")
        idx_ready = per_group("idx_ready", 1)
        gathered = [Count(sem(f"gathered{u}"), 16 * G, 0) for u in range(SLOTS)]
        hot_ready = per_group("hot_ready", 1)
        agg_ready = per_group("agg_ready", G)
        acc_done = per_group("acc_done", G)
        types_hot = per_group("types_hot", 1)
        resets = [Count(sem(f"resets{u}"), 16, 0) for u in range(SLOTS)]
        edge_in = [Count(sem(f"edge_in{u}"), 16 * G, 0) for u in range(SLOTS)]
        hot_turned = per_group("hot_turned", 2)
        turned_copied = per_group("turned_copied", 2)
        er_ready = per_group("er_ready", 1)
        fe_ready = per_group("fe_ready", G)
        fe_added = per_group("fe_added", G)
        score_a = per_group("score_a", 1)
        score_b = per_group("score_b", 1)
        score_turned = per_group("score_turned", 1)
        scan_a = per_group("scan_a", 1)
        scan_b = per_group("scan_b", 1)
        drop_ready = per_group("drop_ready", 1)
        drop_a = per_group("drop_a", 2)
        ref_turned = per_group("ref_turned", 1)
        drop_mm = per_group("drop_mm", 1)
        shifted = per_group("shifted", 1)
        weight_ready = per_group("weight_ready", 1)
        scale_ready = per_group("scale_ready", 1)
        msg_ready = per_group("msg_ready", 2)
        rescaled = per_group("rescaled", 1)
        credited = [idx_ready, hot_ready, agg_ready, acc_done, types_hot, hot_turned, turned_copied, er_ready,
                    fe_ready, fe_added, score_a, score_b, score_turned, scan_a, scan_b, drop_a, drop_ready,
                    ref_turned, drop_mm, shifted, weight_ready, scale_ready, msg_ready, rescaled]
        x_in = Count(sem("x_in"), 16, 0)
        c_turned, c_copied, turned_in, copied_in, products, gates, arg, tanh, used_in, x_new, turned_out, copied_out, \
            table_mm, table_copied = (per_block(n) for n in (
                "c_turned", "c_copied", "turned_in", "copied_in", "products", "gates", "arg", "tanh", "used_in", "x_new",
                "turned_out", "copied_out", "table_mm", "table_copied"))
        gru_a, red_copied = per_block("gru_a"), per_block("red_copied")
        dve_step = Count(sem("dve_step"), 8, 1)
        norm_step = Count(sem("norm_step"), 4, 1)
        rstd = Count(sem("rstd"), 1, 1)
        stored = Count(sem("stored"), 1, 1)
        credited += [c_turned, c_copied, turned_in, copied_in, products, gates, arg, tanh, used_in, x_new, turned_out,
                     copied_out, table_mm, table_copied, dve_step, stored, gru_a, red_copied, norm_step, rstd]
        store_x = Count(sem("store_x"), 16, 0)
        store_t = Count(sem("store_t"), 16, 0)

        prep(nc, a, sb, sem, ps, dict(src_t=src_t, md_t=md_t, type_t=type_t, blk_row=blk_row, tile_row=tile_row,
                                     open_md=open_md, ident=ident, iota=iota, ones=ones, md_lin=md_lin,
                                     rst_dram=rst_dram))
        wts = load_weights(nc, a, sb, sem, ps, ident, ones, credited)

        turned = sb("turned", [P, G, P])
        edge_t = sb("edge_t", [P, SLOTS, G, D])
        score = sb("score", [P, SLOTS, G, H])
        score_raw = sb("score_raw", [P, SLOTS, G, H])
        shift = sb("shift", [P, SLOTS, G, H])
        weight = sb("weight", [P, SLOTS, G, H])
        rst_sb = sb("rst_sb", [H, SLOTS, GE + 1])
        run = sb("run", [H, GE])
        ref = sb("ref", [H, GE])
        carry = sb("carry", [H, SLOTS])
        drop = sb("drop", [H, SLOTS, H])
        dropc = sb("dropc", [H, SLOTS])
        openhot = sb("openhot", [H, SLOTS, P])
        scale = sb("scale", [P, SLOTS, H])
        nsmall = sb("nsmall", [P, BATCH, 2 * H])

        V = dict(locals())
        sum_phase(nc, a, V, a["x"], None)
        node_phase(nc, a, V, "sage", a["x"], x1_dram, None, wts)
        sum_phase(nc, a, V, x1_dram, type_t)
        node_phase(nc, a, V, "gru", x1_dram, x2_dram, (tab_dram[0], wts["w2"]), wts)
        gat_phase(nc, a, V, tab_dram[0], wts["we"])
        node_phase(nc, a, V, "gat", x2_dram, x3_dram, (tab_dram[1], wts["w3a"]), wts)
        gat_phase(nc, a, V, tab_dram[1], None)
        node_phase(nc, a, V, "mid", None, None, (tab_dram[2], wts["w3b"]), wts)
        gat_phase(nc, a, V, tab_dram[2], None)
        node_phase(nc, a, V, "last", x3_dram, a["out"], None, wts)


def prep(nc, a, sb, sem, ps, V):
    ident, iota, ones = V["ident"], V["iota"], V["ones"]
    md_lin, rst_dram = V["md_lin"], V["rst_dram"]
    with ExitStack() as tmp:
        def t(name, shape, dt=F32):
            return tmp.enter_context(nc.sbuf_tensor(name, shape, dt))

        last_i = t("last_i", [BLOCKS, TILES], I32)
        last_f = t("last_f", [BLOCKS, TILES])
        nblk = t("nblk", [P, 1])
        bound = t("bound", [P, 1])
        before = t("before", [BLOCKS, 1])
        turn_at = t("turn_at", [BLOCKS, 1])
        kio = t("kio", [P, KPAD])
        past = t("past", [BLOCKS, KPAD])
        bcol = t("bcol", [P, CHUNKS])
        kcol = t("kcol", [P, CHUNKS])
        tcol_f = t("tcol_f", [P, CHUNKS])
        tcol = t("tcol", [P, CHUNKS], I32)
        row_i = t("row_i", [P, 3, CHUNKS, P], I32)
        row_f = t("row_f", [P, 3, CHUNKS, P])
        rel = t("rel", [P, CHUNKS, P])
        m1 = t("m1_", [P, CHUNKS, P])
        md = t("md_rows", [P, CHUNKS, P])
        pad = t("pad", [1, 2])
        before_md = t("before_md", [P, CHUNKS, P])
        op = t("op", [H, 2, GROUPS + 1])
        brow_f = t("brow_f", [1, KPAD])
        trow_f = t("trow_f", [1, KPAD])
        ld, io, vv, pe, g_in, st, l2, st2, l3 = (sem(f"prep_{n}") for n in
                                                 ("load", "iota", "vec", "pe", "gather", "store", "shifted", "rst", "open"))
        with nc.Block() as block:
            @block.sync
            def _(sp):
                sp.dma_start(last_i[:, :], a["dlast"].rearrange("(a n) -> a n", a=1).to_broadcast([BLOCKS, TILES])).then_inc(ld, 16)
                sp.dma_start(ident[:, :], a["ident"]).then_inc(ld, 16)
                sp.dma_start(kio[:, :], a["kio"].rearrange("(a n) -> a n", a=1).to_broadcast([P, KPAD])).then_inc(ld, 16)
                sp.dma_start(kcol[:, :], a["kcol"]).then_inc(ld, 16)
                sp.dma_start(nblk[:, :], a["pcol"]).then_inc(ld, 16)
                sp.wait_ge(vv, 10)
                with nc.allow_non_contiguous_dma(reason="pads"):
                    sp.dma_start(md_lin[1:1 + KPAD * P].rearrange("(c p e) -> p c e", c=CHUNKS, e=P), md[:, :, :]).then_inc(st, 16)
                    sp.dma_start(md_lin[0:1].rearrange("(a n) -> a n", a=1), pad[0:1, 0:1]).then_inc(st, 16)
                    sp.wait_ge(st, 32)
                    sp.dma_start(before_md[:, :, :], md_lin[0:KPAD * P].rearrange("(c p e) -> p c e", c=CHUNKS, e=P)).then_inc(l2, 16)
                    for n in range(2):
                        first = md_lin[1 - n:1 - n + (GROUPS + 1) * GE].rearrange("(g e) -> g e", e=GE)[:, 0:1]
                        sp.dma_start(op[:, n, :], first.rearrange("g a -> a g").to_broadcast([H, GROUPS + 1])).then_inc(l3, 16)
                    sp.wait_ge(vv, 12)
                    sp.dma_start(rst_dram.rearrange("(c p e) -> p c e", c=CHUNKS, e=P), before_md[:, :, :]).then_inc(st2, 16)
                    sp.wait_ge(st2, 16)

            @block.gpsimd
            def _(pool):
                pool.wait_ge(vv, 7)
                for n, tab in enumerate((a["src"], a["dst"], a["etype"])):
                    for c in range(CHUNKS):
                        pool.indirect_dma_start(out=row_i[:, n, c, :], out_offset=None, in_=tab,
                                                in_offset=bass.IndirectOffsetOnAxis(ap=tcol[:, c:c + 1], axis=0)).then_inc(g_in, 16)
                pool.wait_ge(g_in, 16 * 3 * CHUNKS)

            @block.tensor
            def _(te):
                te.wait_ge(vv, 4)
                half = KPAD // 2
                for n in range(2):
                    te.matmul(ps[0:1, n, 0:half], ones[0:BLOCKS - 1, 0:1], past[0:BLOCKS - 1, n * half:(n + 1) * half], start=True, stop=True)
                for c in range(CHUNKS):
                    mm = te.matmul(ps[:, 2, c:c + 1], past[0:BLOCKS - 1, c * P:(c + 1) * P], ones[0:BLOCKS - 1, 0:1], start=True, stop=True)
                mm.then_inc(pe, 1)
                te.wait_ge(vv, 10)
                for n in range(3):
                    src = (row_f[:, 0], md, row_f[:, 2])[n]
                    for c in range(CHUNKS):
                        bank, at = 3 + (n * CHUNKS + c) // 4 % 5, (n * CHUNKS + c) % 4
                        if n * CHUNKS + c >= 20 and at == 0:
                            te.wait_ge(vv, 14)
                        te.transpose(ps[:, bank, at * P:(at + 1) * P], src[:, c, :], ident[:, :]).then_inc(pe, 1)

            @block.vector
            def _(v):
                v.memset(ones[:, :], 1.0)
                v.memset(pad[:, :], -7.0)
                v.wait_ge(ld, 16 * 5)
                v.tensor_copy(iota[:, :], kio[:, 0:P])
                v.tensor_scalar(bound[:, :], nblk[:, :], float(P), float(P), ALU.mult, ALU.add).then_inc(vv, 1)
                v.tensor_copy(last_f[:, :], last_i[:, :]).then_inc(vv, 1)
                v.wait_ge(vv, 2)
                v.tensor_scalar(last_f[:, :], last_f[:, :], bound[0:BLOCKS, 0:1], None, ALU.is_lt).then_inc(vv, 1)
                v.wait_ge(vv, 3)
                v.reduce_sum(before[:, :], last_f[:, :], mybir.AxisListType.X).then_inc(io, 1)
                v.wait_ge(io, 1)
                v.tensor_scalar(turn_at[:, :], before[:, :], nblk[0:BLOCKS, 0:1], 1.0, ALU.add, ALU.add).then_inc(io, 1)
                v.wait_ge(io, 2)
                v.tensor_scalar(past[:, :], kio[0:BLOCKS, :], turn_at[:, 0:1], None, ALU.is_ge).then_inc(vv, 1)
                v.wait_ge(pe, 1)
                v.tensor_copy(bcol[:, :], ps[:, 2, 0:CHUNKS]).then_inc(vv, 1)
                half = KPAD // 2
                for n in range(2):
                    v.tensor_copy(brow_f[:, n * half:(n + 1) * half], ps[0:1, n, 0:half])
                v.tensor_tensor(tcol_f[:, :], kcol[:, :], ps[:, 2, 0:CHUNKS], ALU.subtract).then_inc(vv, 1)
                v.wait_ge(vv, 6)
                v.tensor_scalar(tcol[:, :], tcol_f[:, :], float(TILES), None, ALU.min).then_inc(vv, 1)
                v.tensor_tensor(trow_f[:, :], kio[0:1, :], brow_f[:, :], ALU.subtract).then_inc(io, 1)
                v.tensor_copy(V["blk_row"][:, :], brow_f[:, :])
                v.wait_ge(io, 3)
                v.tensor_scalar(V["tile_row"][:, :], trow_f[:, :], float(TILES), None, ALU.min)
                v.wait_ge(g_in, 16 * 3 * CHUNKS)
                v.tensor_copy(row_f[:, :, :, :], row_i[:, :, :, :]).then_inc(vv, 1)
                v.tensor_scalar(bcol[:, :], bcol[:, :], float(P), None, ALU.mult).then_inc(io, 1)
                v.wait_ge(vv, 8)
                v.wait_ge(io, 4)
                for c in range(CHUNKS):
                    v.tensor_scalar(rel[:, c, :], row_f[:, 1, c, :], bcol[:, c:c + 1], None, ALU.subtract).then_inc(io, 1)
                v.wait_ge(io, 4 + CHUNKS)
                v.tensor_scalar(m1[:, :, :], rel[:, :, :], 0.0, None, ALU.is_ge).then_inc(io, 1)
                v.wait_ge(io, 5 + CHUNKS)
                v.scalar_tensor_tensor(out=m1[:, :, :], in0=rel[:, :, :], scalar=float(P - 1), in1=m1[:, :, :], op0=ALU.is_le, op1=ALU.mult).then_inc(vv, 1)
                v.wait_ge(vv, 9)
                v.scalar_tensor_tensor(out=md[:, :, :], in0=rel[:, :, :], scalar=1.0, in1=m1[:, :, :], op0=ALU.add, op1=ALU.mult).then_inc(io, 1)
                v.wait_ge(io, 6 + CHUNKS)
                v.tensor_scalar(md[:, :, :], md[:, :, :], -1.0, None, ALU.add).then_inc(vv, 1)
                v.wait_ge(vv, 10)
                v.wait_ge(l2, 16)
                v.tensor_tensor(before_md[:, :, :], before_md[:, :, :], md[:, :, :], ALU.not_equal).then_inc(vv, 1)
                v.wait_ge(vv, 11)
                v.tensor_scalar(before_md[:, :, :], before_md[:, :, :], -BIG, None, ALU.mult).then_inc(vv, 1)
                v.wait_ge(l3, 32)
                v.tensor_tensor(op[:, 1, :], op[:, 0, :], op[:, 1, :], ALU.is_equal).then_inc(io, 1)
                v.wait_ge(io, 7 + CHUNKS)
                v.scalar_tensor_tensor(out=V["open_md"][:, :], in0=op[:, 0, :], scalar=1.0, in1=op[:, 1, :], op0=ALU.add, op1=ALU.mult).then_inc(io, 1)
                v.wait_ge(io, 8 + CHUNKS)
                v.tensor_scalar(V["open_md"][:, :], V["open_md"][:, :], -1.0, None, ALU.add)
                outs = (V["src_t"], V["md_t"], V["type_t"])

                def turn_out(j):
                    n, c = j // CHUNKS, j % CHUNKS
                    return v.tensor_copy(outs[n][:, c * P:(c + 1) * P], ps[:, 3 + j // 4 % 5, j % 4 * P:(j % 4 + 1) * P])

                v.wait_ge(pe, 1 + 20)
                for j in range(20):
                    turn_out(j).then_inc(io, 1)
                v.wait_ge(io, 28 + CHUNKS)
                v.engine_nop().then_inc(vv, 2)
                v.wait_ge(pe, 1 + 3 * CHUNKS)
                for j in range(20, 3 * CHUNKS):
                    turn_out(j)


def load_weights(nc, a, sb, sem, ps, ident, ones, credited):
    w = {}
    for name in ("ws", "wn"):
        w[name] = sb(name, [P, 2, D])
    for name in ("wih", "whh"):
        w[name] = sb(name, [P, 2, 3 * D])
    w["rel"] = sb("relv", [NREL, D])
    for name in ("w2", "we", "w3a", "w3b"):
        w[name] = sb(name, [P, 2, FW + 2 * H])
    rowsb = {"b0": D, "bih": 3 * D, "bhh": 3 * D, "b2": D, "b3a": D, "b3b": D}
    for name, n in rowsb.items():
        w[name] = sb(name, [1, n])
    w["brz"] = sb("brz", [1, 2 * D])
    for name in ("b2", "b3a", "b3b"):
        w[name + "_all"] = sb(name + "_all", [P, D])
    ld, on, pe, dv = (sem(f"weights_{n}") for n in ("load", "spread", "turned", "copied"))
    with ExitStack() as tmp:
        def t(name, shape):
            return tmp.enter_context(nc.sbuf_tensor(name, shape, F32))

        nat = {name: t(name + "_nat", [P, 2, D]) for name in ("w2", "we", "w3a", "w3b")}
        tr = {name: t(name + "_tr", [P, 2, D]) for name in ("w2", "we", "w3a", "w3b")}
        mask = t("headmask", [P, 2, H])
        cols = {"w2": ("al2", "ar2"), "we": ("ae2",), "w3a": ("al3a", "ar3a"), "w3b": ("al3b", "ar3b")}
        vec, spread = {}, {}
        for name, vs in cols.items():
            for x in vs:
                vec[x] = t(x + "_v", [P, 2])
                spread[x] = t(x + "_s", [P, 2, H])
        total = 0
        with nc.Block() as block:
            @block.sync
            def _(sp):
                nonlocal total
                loads = [(w[n][:, :, :], a[n].rearrange("(c p) n -> p c n", p=P)) for n in ("ws", "wn", "wih", "whh")]
                for n in nat:
                    loads.append((nat[n][:, :, :], a[n].rearrange("(c p) n -> p c n", p=P)))
                    loads.append((tr[n][:, :, :], a[n + "_t"].rearrange("(c p) n -> p c n", p=P)))
                loads.append((w["rel"][:, :], a["rel"]))
                loads += [(w[n][:, :], a[n].rearrange("(a n) -> a n", a=1)) for n in rowsb]
                loads += [(w[n + "_all"][:, :], a[n].rearrange("(a n) -> a n", a=1).to_broadcast([P, D])) for n in ("b2", "b3a", "b3b")]
                loads.append((mask[:, :, :], a["headmask"].rearrange("(c p) n -> p c n", p=P)))
                with nc.allow_non_contiguous_dma(reason="small vectors"):
                    loads += [(vec[x][:, :], a[x].rearrange("(c p) -> p c", p=P)) for x in vec]
                    for o, i in loads:
                        sp.dma_start(o, i).then_inc(ld, 16)
                total = 16 * len(loads)
                for c in credited:
                    sp.sem_inc(c.h, c.base)

            @block.vector
            def _(v):
                v.wait_ge(ld, total)
                for name in nat:
                    v.memset(w[name][:, :, :], 0.0).then_inc(dv, 1)
                v.wait_ge(dv, 4)
                for name in nat:
                    for c in range(2):
                        v.tensor_copy(w[name][:, c, 0:FW].rearrange("p (h d) -> p h d", h=H)[:, :, 0:HD],
                                      nat[name][:, c, :].rearrange("p (h d) -> p h d", h=H))
                v.tensor_tensor(w["brz"][:, :], w["bih"][:, 0:2 * D], w["bhh"][:, 0:2 * D], ALU.add)
                for x in vec:
                    for c in range(2):
                        v.tensor_scalar(spread[x][:, c, :], mask[:, c, :], vec[x][:, c:c + 1], None, ALU.mult).then_inc(on, 1)
                v.wait_ge(pe, 1)
                at = 0
                for name, vs in cols.items():
                    for j, x in enumerate(vs):
                        for c in range(2):
                            v.tensor_copy(w[name][:, c, FW + j * H:FW + (j + 1) * H], ps[:, 0, at:at + H])
                            at += H

            @block.tensor
            def _(te):
                te.wait_ge(on, 2 * len(vec))
                at = 0
                for name, vs in cols.items():
                    for x in vs:
                        for c in range(2):
                            for k in range(2):
                                mm = te.matmul(ps[:, 0, at:at + H], tr[name][:, k, c * P:(c + 1) * P], spread[x][:, k, :],
                                               start=(k == 0), stop=(k == 1))
                            at += H
                mm.then_inc(pe, 1)
    return w


def settle(eng, V):
    eng.sem_inc(V["settled"], 1)


def numbers_of(nc, engine, table, g, most):
    _, vals = nc.values_load_multi_w_load_instructions(
        table[0:1, bass.ds(g * G, G)], engines=[engine], min_val=0, max_val=most,
        skip_runtime_bounds_check_because="the table's values are counts of at most BLOCKS - 1 turns, or a minimum with TILES")
    return vals


def gather_rows(nc, V, table, width, used, extra):
    def body(pool):
        def group(g, u):
            pool.wait_ge(used.h, used.at(g - SLOTS))
            pool.tensor_copy(V["idx"][:, u, :], V["src_t"][:, bass.ds(g * G, G)]).then_inc(V["idx_ready"].h, 1)
            pool.wait_ge(V["idx_ready"].h, V["idx_ready"].at(g))
            settle(pool, V)
            for k in range(G):
                pool.indirect_dma_start(out=V["rows"][:, u, k, 0:width], out_offset=None, in_=table,
                                        in_offset=bass.IndirectOffsetOnAxis(ap=V["idx"][:, u, k:k + 1], axis=0)
                                        ).then_inc(V["gathered"][u].h, 16)

        with pool.Fori(0, LOOPS) as i:
            for u in range(SLOTS):
                group(i * SLOTS + u, u)
        for g in range(GROUPS, GROUPS + extra):
            group(g, g % SLOTS)
    return body


def make_hot(v, V, g, u):
    v.wait_ge(V["agg_ready"].h, V["agg_ready"].at(g - SLOTS))
    for k in range(G):
        op = v.tensor_scalar(V["hot"][:, u, k, :], V["iota"][:, :], V["md_t"][:, bass.ds(g * G + k, 1)], None, ALU.is_equal)
    op.then_inc(V["hot_ready"].h, 1)


def sum_phase(nc, a, V, table, types):
    ps, rows, acc, hot = V["ps"], V["rows"], V["acc"], V["hot"]
    width = D + (NREL if types is not None else 1)
    hot_ready, agg_ready, acc_done, gathered, types_hot = (V[n] for n in ("hot_ready", "agg_ready", "acc_done", "gathered", "types_hot"))
    cleared, start = V["cleared"], 2 if types is None else 1
    with nc.Block() as block:
        block.gpsimd(gather_rows(nc, V, table, D, agg_ready, 0))

        @block.vector
        def _(v):
            v.memset(acc[:, :, :], 0.0).then_inc(cleared.h, 1)
            if types is None:
                v.memset(rows[:, :, :, D:D + 1], 1.0).then_inc(cleared.h, 1)
            v.wait_ge(cleared.h, cleared.at(0, start))
            make_hot(v, V, 0, 0)
            with v.Fori(0, LOOPS) as i:
                for u in range(SLOTS):
                    g = i * SLOTS + u
                    if types is not None:
                        for k in range(G):
                            op = v.tensor_scalar(rows[:, u, k, D:D + NREL], V["iota"][:, 0:NREL], types[:, bass.ds(g * G + k, 1)], None, ALU.is_equal)
                        op.then_inc(types_hot.h, 1)
                    make_hot(v, V, g + 1, (u + 1) % SLOTS)
                    blk = numbers_of(nc, ENG.DVE, V["blk_row"], g, BLOCKS - 1)
                    for k in range(G):
                        v.wait_ge(agg_ready.h, agg_ready.at(g, k + 1))
                        v.wait_ge(acc_done.h, acc_done.at(g, k))
                        to = acc[:, bass.ds(blk[k], 1), 0:width].rearrange("p a w -> p (a w)")
                        v.tensor_tensor(to, to, ps[:, k % 8, 0:width], ALU.add).then_inc(acc_done.h, 1)
            v.wait_ge(acc_done.h, acc_done.at(GROUPS - 1))

        @block.tensor
        def _(te):
            te.wait_ge(cleared.h, cleared.at(0, start))
            with te.Fori(0, LOOPS) as i:
                for u in range(SLOTS):
                    g = i * SLOTS + u
                    te.wait_ge(gathered[u].h, gathered[u].at(i))
                    te.wait_ge(hot_ready.h, hot_ready.at(g))
                    if types is not None:
                        te.wait_ge(types_hot.h, types_hot.at(g))
                    for k in range(G):
                        te.wait_ge(acc_done.h, acc_done.at(g - 1, k + 1))
                        te.matmul(ps[:, k % 8, 0:width], hot[:, u, k, :], rows[:, u, k, 0:width], start=True, stop=True).then_inc(agg_ready.h, 1)
    cleared.base += start
    if types is not None:
        types_hot.phase_ended(GROUPS)
    hot_ready.phase_ended(GROUPS + 1)
    agg_ready.phase_ended(GROUPS)
    acc_done.phase_ended(GROUPS)
    V["idx_ready"].phase_ended(GROUPS)
    for c in gathered:
        c.phase_ended(LOOPS)


def gat_phase(nc, a, V, table, we):
    (ps, rows, acc, hot, turned, edge_t, score, score_raw, shift, weight, rst_sb, run, ref, carry, drop, dropc, openhot, scale,
     er_sb, ident, iota) = (V[n] for n in (
         "ps", "rows", "acc", "hot", "turned", "edge_t", "score", "score_raw", "shift", "weight", "rst_sb", "run",
         "ref", "carry", "drop", "dropc", "openhot", "scale", "er_sb", "ident", "iota"))
    cleared, gathered, resets, edge_in = (V[n] for n in ("cleared", "gathered", "resets", "edge_in"))
    (hot_ready, agg_ready, acc_done, hot_turned, turned_copied, er_ready, fe_ready, fe_added, score_a, score_b,
     score_turned, scan_a, scan_b, drop_a, drop_ready, ref_turned, drop_mm, shifted, weight_ready, scale_ready, msg_ready,
     rescaled) = (V[n] for n in (
         "hot_ready", "agg_ready", "acc_done", "hot_turned", "turned_copied", "er_ready", "fe_ready", "fe_added",
         "score_a", "score_b", "score_turned", "scan_a", "scan_b", "drop_a", "drop_ready", "ref_turned", "drop_mm", "shifted",
         "weight_ready", "scale_ready", "msg_ready", "rescaled"))
    BANK_HOT, BANK_SMALL, BANK_SCORE, BANK_SUM, BANK_FE = 0, 1, 2, 4, 6
    SUMS = 2 if we is not None else 4
    er_ps = ps[:, BANK_SMALL, 0:G * H]
    ref_ps = ps[:, BANK_SMALL, G * H:2 * G * H]
    drop_ps = ps[:, BANK_HOT, 0:H]
    score_ps = ps[0:H, BANK_SCORE:BANK_SCORE + 2, :].rearrange("h b e -> h (b e)")

    def heads(ap):
        return ap.rearrange("p (h d) -> p h d", h=H)

    with nc.Block() as block:
        block.gpsimd(gather_rows(nc, V, table, ROW, agg_ready, 1))

        @block.sync
        def _(sp):
            def edges(g, u):
                tile = numbers_of(nc, ENG.SP, V["tile_row"], g, TILES)
                sp.wait_ge(fe_ready.h, fe_ready.at(g - SLOTS))
                settle(sp, V)
                for k in range(G):
                    sp.dma_start(edge_t[:, u, k, :], a["edge"][bass.ds(tile[k], 1), :, :].rearrange("a p n -> (a p) n")).then_inc(edge_in[u].h, 16)

            with sp.Fori(0, LOOPS) as i:
                for u in range(SLOTS):
                    g = i * SLOTS + u
                    sp.wait_ge(scan_b.h, scan_b.at(g - SLOTS))
                    settle(sp, V)
                    sp.dma_start(rst_sb[:, u, :], V["rst_dram"][bass.ds(g * GE, GE + 1)].rearrange("(a e) -> a e", a=1).to_broadcast([H, GE + 1])).then_inc(resets[u].h, 16)
                    if we is not None:
                        edges(g, u)
            if we is not None:
                edges(GROUPS, GROUPS % SLOTS)

        @block.vector
        def _(v):
            def add_edge_part(g, u, i):
                v.wait_ge(gathered[u].h, gathered[u].at(i))
                for k in range(G):
                    v.wait_ge(fe_ready.h, fe_ready.at(g, k + 1))
                    v.tensor_tensor(rows[:, u, k, :], rows[:, u, k, :], ps[:, BANK_FE + k % 2, 0:ROW], ALU.add).then_inc(fe_added.h, 1)
                v.wait_ge(fe_added.h, fe_added.at(g))

            def scores(g, u, i):
                v.wait_ge(er_ready.h, er_ready.at(g))
                v.wait_ge(gathered[u].h, gathered[u].at(i))
                v.tensor_tensor(score_raw[:, u, :, :], rows[:, u, :, FW:ROW], er_ps.rearrange("p (g h) -> p g h", g=G), ALU.add).then_inc(score_a.h, 1)
                v.wait_ge(score_a.h, score_a.at(g))
                v.scalar_tensor_tensor(out=score[:, u, :, :], in0=score_raw[:, u, :, :], scalar=SLOPE, in1=score_raw[:, u, :, :], op0=ALU.mult, op1=ALU.max).then_inc(score_b.h, 1)

            v.memset(acc[:, :, :], 0.0).then_inc(cleared.h, 1)
            v.memset(carry[:, :], -BIG).then_inc(cleared.h, 1)
            v.wait_ge(cleared.h, cleared.at(0, 2))
            make_hot(v, V, 0, 0)
            if we is not None:
                add_edge_part(0, 0, 0)
            scores(0, 0, 0)
            with v.Fori(0, LOOPS) as i:
                for u in range(SLOTS):
                    g, prev, nxt = i * SLOTS + u, (u - 1) % SLOTS, (u + 1) % SLOTS
                    nxt_i = i + 1 if nxt == 0 else i
                    v.wait_ge(resets[u].h, resets[u].at(i))
                    v.wait_ge(score_turned.h, score_turned.at(g))
                    v.tensor_tensor_scan(run[:, :], rst_sb[:, u, 0:GE], score_ps, carry[:, prev:prev + 1], ALU.add, ALU.max).then_inc(scan_a.h, 1)
                    v.wait_ge(scan_a.h, scan_a.at(g))
                    v.wait_ge(ref_turned.h, ref_turned.at(g - 1))
                    v.tensor_copy(carry[:, u:u + 1], run[:, GE - 1:GE]).then_inc(drop_a.h, 1)
                    v.tensor_tensor_scan(ref[:, ::-1], rst_sb[:, u, GE:0:-1], run[:, ::-1], -BIG, ALU.add, ALU.max).then_inc(scan_b.h, 1)
                    v.wait_ge(scan_b.h, scan_b.at(g))
                    v.tensor_tensor(dropc[:, u:u + 1], carry[:, prev:prev + 1], ref[:, 0:1], ALU.subtract).then_inc(drop_a.h, 1)
                    v.tensor_scalar(openhot[:, u, :], iota[0:H, :], V["open_md"][:, bass.ds(g, 1)], None, ALU.is_equal)
                    v.wait_ge(drop_a.h, drop_a.at(g))
                    v.tensor_scalar(drop[:, u, :], ident[0:H, 0:H], dropc[:, u:u + 1], None, ALU.mult).then_inc(drop_ready.h, 1)
                    make_hot(v, V, g + 1, nxt)
                    v.wait_ge(ref_turned.h, ref_turned.at(g))
                    v.tensor_tensor(shift[:, u, :, :], score[:, u, :, :], ref_ps.rearrange("p (g h) -> p g h", g=G), ALU.subtract).then_inc(shifted.h, 1)
                    if we is not None:
                        add_edge_part(g + 1, nxt, nxt_i)
                    v.wait_ge(weight_ready.h, weight_ready.at(g))
                    for n in range(2):
                        part = rows[:, u, n * G // 2:(n + 1) * G // 2, 0:FW].rearrange("p g (h d) -> p g h d", h=H)
                        v.tensor_tensor(part, part, weight[:, u, n * G // 2:(n + 1) * G // 2, :].unsqueeze(3).to_broadcast([P, G // 2, H, HW]), ALU.mult).then_inc(msg_ready.h, 1)
                    blk = numbers_of(nc, ENG.DVE, V["blk_row"], g, BLOCKS - 1)
                    v.wait_ge(scale_ready.h, scale_ready.at(g))
                    v.wait_ge(acc_done.h, acc_done.at(g - 1))
                    to = heads(acc[:, bass.ds(blk[0], 1), 0:FW].rearrange("p a w -> p (a w)"))
                    v.tensor_tensor(to, to, scale[:, u, :].unsqueeze(2).to_broadcast([P, H, HW]), ALU.mult).then_inc(rescaled.h, 1)
                    scores(g + 1, nxt, nxt_i)
                    v.wait_ge(rescaled.h, rescaled.at(g))
                    for k in range(G):
                        v.wait_ge(agg_ready.h, agg_ready.at(g, k + 1))
                        v.wait_ge(acc_done.h, acc_done.at(g, k))
                        to = acc[:, bass.ds(blk[k], 1), 0:FW].rearrange("p a w -> p (a w)")
                        v.tensor_tensor(to, to, ps[:, BANK_SUM + k % SUMS, 0:FW], ALU.add).then_inc(acc_done.h, 1)
            v.wait_ge(acc_done.h, acc_done.at(GROUPS - 1))

        @block.tensor
        def _(te):
            def turn_hot(g, u):
                te.wait_ge(hot_ready.h, hot_ready.at(g))
                te.wait_ge(scale_ready.h, scale_ready.at(g - 1))
                for n in range(2):
                    te.wait_ge(turned_copied.h, turned_copied.at(g, n))
                    for k in range(G // 2):
                        mm = te.transpose(ps[:, BANK_HOT, k * P:(k + 1) * P], hot[:, u, n * G // 2 + k, :], ident[:, :])
                    mm.then_inc(hot_turned.h, 1)

            def er_of(g, u):
                blk = numbers_of(nc, ENG.PE, V["blk_row"], g, BLOCKS - 1)
                te.wait_ge(score_a.h, score_a.at(g - 1))
                te.wait_ge(shifted.h, shifted.at(g - 1))
                te.wait_ge(turned_copied.h, turned_copied.at(g))
                for k in range(G):
                    mm = te.matmul(ps[:, BANK_SMALL, k * H:(k + 1) * H], turned[:, k, :], er_sb[:, bass.ds(blk[k] * H, H)], start=True, stop=True)
                mm.then_inc(er_ready.h, 1)

            def project_edges(g, u, i):
                te.wait_ge(edge_in[u].h, edge_in[u].at(i))
                for k in range(G):
                    te.wait_ge(fe_added.h, fe_added.at(g, k - 1))
                    for c in range(2):
                        mm = te.matmul(ps[:, BANK_FE + k % 2, 0:ROW], edge_t[:, u, k, c * P:(c + 1) * P], we[:, c, 0:ROW], start=(c == 0), stop=(c == 1))
                    mm.then_inc(fe_ready.h, 1)

            def turn_scores(g, u):
                te.wait_ge(score_b.h, score_b.at(g))
                te.wait_ge(scan_a.h, scan_a.at(g - 1))
                for k in range(G):
                    mm = te.transpose(score_ps[:, k * P:(k + 1) * P], score[:, u, k, :], ident[:, :])
                mm.then_inc(score_turned.h, 1)

            def sums(g, u, ks):
                for k in ks:
                    te.wait_ge(acc_done.h, acc_done.at(g, k - SUMS + 1))
                    te.matmul(ps[:, BANK_SUM + k % SUMS, 0:FW], hot[:, u, k, :], rows[:, u, k, 0:FW], start=True, stop=True).then_inc(agg_ready.h, 1)

            turn_hot(0, 0)
            er_of(0, 0)
            if we is not None:
                project_edges(0, 0, 0)
            turn_scores(0, 0)
            with te.Fori(0, LOOPS) as i:
                for u in range(SLOTS):
                    g, nxt = i * SLOTS + u, (u + 1) % SLOTS
                    te.wait_ge(scan_b.h, scan_b.at(g))
                    te.wait_ge(shifted.h, shifted.at(g - 1))
                    te.wait_ge(score_a.h, score_a.at(g))
                    settle(te, V)
                    for k in range(G):
                        mm = te.transpose(ps[:, BANK_SMALL, G * H + k * H:G * H + (k + 1) * H], ref[:, k * P:(k + 1) * P], ident[0:H, 0:H])
                    mm.then_inc(ref_turned.h, 1)
                    te.wait_ge(drop_ready.h, drop_ready.at(g))
                    te.wait_ge(turned_copied.h, turned_copied.at(g))
                    te.matmul(drop_ps, openhot[:, u, :], drop[:, u, :], start=True, stop=True).then_inc(drop_mm.h, 1)
                    turn_hot(g + 1, nxt)
                    er_of(g + 1, nxt)
                    if we is not None:
                        project_edges(g + 1, nxt, i + 1 if nxt == 0 else i)
                    te.wait_ge(msg_ready.h, msg_ready.at(g, 1))
                    sums(g, u, range(2))
                    turn_scores(g + 1, nxt)
                    sums(g, u, range(2, G // 2))
                    te.wait_ge(msg_ready.h, msg_ready.at(g))
                    sums(g, u, range(G // 2, G))

        @block.scalar
        def _(act):
            def copy_turned(g, u):
                for n in range(2):
                    act.wait_ge(hot_turned.h, hot_turned.at(g, n + 1))
                    act.wait_ge(er_ready.h, er_ready.at(g - 1))
                    act.copy(turned[:, n * G // 2:(n + 1) * G // 2, :].rearrange("p g e -> p (g e)"), ps[:, BANK_HOT, :]).then_inc(turned_copied.h, 1)

            copy_turned(0, 0)
            with act.Fori(0, LOOPS) as i:
                for u in range(SLOTS):
                    g, nxt = i * SLOTS + u, (u + 1) % SLOTS
                    act.wait_ge(drop_mm.h, drop_mm.at(g))
                    act.activation(scale[:, u, :], drop_ps, ACT.Exp).then_inc(scale_ready.h, 1)
                    act.wait_ge(shifted.h, shifted.at(g))
                    act.activation(weight[:, u, :, :], shift[:, u, :, :], ACT.Exp).then_inc(weight_ready.h, 1)
                    copy_turned(g + 1, nxt)

    cleared.base += 2
    for c in (hot_ready, hot_turned, turned_copied, er_ready, score_a, score_b, score_turned, V["idx_ready"]):
        c.phase_ended(GROUPS + 1)
    for c in (agg_ready, acc_done, scan_a, scan_b, drop_a, drop_ready, ref_turned, drop_mm, shifted, weight_ready,
              scale_ready, msg_ready, rescaled):
        c.phase_ended(GROUPS)
    for u in range(SLOTS):
        more = 1 if u < (GROUPS + 1) - LOOPS * SLOTS else 0
        gathered[u].phase_ended(LOOPS + more)
        resets[u].phase_ended(LOOPS)
        if we is not None:
            edge_in[u].phase_ended(LOOPS + more)
    if we is not None:
        fe_ready.phase_ended(GROUPS + 1)
        fe_added.phase_ended(GROUPS + 1)


def node_phase(nc, a, V, kind, x_dram, out_dram, table, w):
    ps, acc, ident, ones, er_sb = (V[n] for n in ("ps", "acc", "ident", "ones", "er_sb"))
    (x_in, c_turned, c_copied, turned_in, copied_in, products, gates, arg, tanh, used_in, x_new, turned_out, copied_out,
     table_mm, table_copied, dve_step, stored, store_x, store_t, red_copied, gru_a, norm_step, rstd) = (V[n] for n in (
         "x_in", "c_turned", "c_copied", "turned_in", "copied_in", "products", "gates", "arg", "tanh", "used_in",
         "x_new", "turned_out", "copied_out", "table_mm", "table_copied", "dve_step", "stored", "store_x", "store_t", "red_copied", "gru_a", "norm_step", "rstd"))
    flat = {n: V[n][:, :, :, :].rearrange("p a b c -> p (a b c)") for n in ("rows", "edge_t", "hot")}

    def part(buf, at, width):
        return flat[buf][:, at:at + BATCH * width].rearrange("p (i d) -> p i d", i=BATCH)

    tin = part("rows", 0, 2 * D)
    tab = part("rows", BATCH * 2 * D, ROW)
    y = part("edge_t", 0, D)
    pre = part("edge_t", BATCH * D, D)
    xin = part("edge_t", 2 * BATCH * D, D)
    zg = part("hot", 0, D)
    ct = part("hot", BATCH * D, P)
    rg = tin[:, :, D:2 * D]
    small = V["nsmall"]
    rec, stats, mv = small[:, :, 0:H], small[:, :, H:H + 6], small[:, :, H + 6:H + 8]
    project = kind in ("sage", "gru")
    norm = kind != "mid"
    need_x = x_dram is not None
    tdram, wt = table if table else (None, None)

    def heads(ap):
        return ap.rearrange("p (h d) -> p h d", h=H)

    with nc.Block() as block:
        @block.sync
        def _(sp):
            with sp.Fori(0, NBATCH) as i:
                if need_x:
                    sp.wait_ge(x_new.h, x_new.at(i * BATCH - 1))
                    settle(sp, V)
                    sp.dma_start(xin, x_dram[bass.ds(i * (BATCH * P), BATCH * P), :].rearrange("(b p) d -> p b d", p=P)).then_inc(x_in.h, 16)
                if out_dram is not None:
                    sp.wait_ge(x_new.h, x_new.at(i * BATCH + BATCH - 1))
                    settle(sp, V)
                    sp.dma_start(out_dram[bass.ds(i * (BATCH * P), BATCH * P), :].rearrange("(b p) d -> p b d", p=P), y).then_inc(store_x.h, 16)
                if table:
                    sp.wait_ge(table_copied.h, table_copied.at(i * BATCH + BATCH - 1))
                    settle(sp, V)
                    sp.dma_start(tdram[bass.ds(i * (BATCH * P), BATCH * P), :].rearrange("(b p) d -> p b d", p=P), tab).then_inc(store_t.h, 16)
                    sp.wait_ge(store_t.h, store_t.at(i))
                    settle(sp, V)
                if out_dram is not None:
                    sp.wait_ge(store_x.h, store_x.at(i))
                sp.sem_inc(stored.h, 1)

        @block.vector
        def _(v):
            if table:
                for j in range(BATCH):
                    op = v.memset(heads(tab[:, j, 0:FW])[:, :, HD:HW], 1.0)
                op.then_inc(V["cleared"].h, 1)
            with v.Fori(0, NBATCH) as i:
                step = [0]

                def block_of(j):
                    return bass.ds(i * BATCH + j, 1)

                def one(ap):
                    return ap.rearrange("p a w -> p (a w)")

                def ended(op):
                    op.then_inc(dve_step.h, 1)
                    step[0] += 1
                    v.wait_ge(dve_step.h, dve_step.at(i, step[0]))

                js = range(BATCH)
                v.wait_ge(x_new.h, x_new.at(i * BATCH - 1))
                if kind == "sage":
                    for j in js:
                        op = v.tensor_scalar(rec[:, j, 0:1], one(acc[:, block_of(j), D:D + 1]), 1.0, None, ALU.max)
                    ended(op)
                    for j in js:
                        op = v.reciprocal(rec[:, j, 0:1], rec[:, j, 0:1])
                    ended(op)
                    for j in js:
                        v.tensor_scalar(pre[:, j, :], one(acc[:, block_of(j), 0:D]), rec[:, j, 0:1], None, ALU.mult).then_inc(arg.h, 1)
                if kind in ("gat", "mid", "last"):
                    for j in js:
                        op = v.tensor_scalar(rec[:, j, :].unsqueeze(2), heads(one(acc[:, block_of(j), 0:FW]))[:, :, HD:HW], 0.5, None, ALU.max)
                    ended(op)
                    for j in js:
                        op = v.reciprocal(rec[:, j, :], rec[:, j, :])
                    ended(op)
                    for j in js:
                        op = v.tensor_tensor(heads(pre[:, j, :]), heads(one(acc[:, block_of(j), 0:FW]))[:, :, 0:HD],
                                             rec[:, j, :].unsqueeze(2).to_broadcast([P, H, HD]), ALU.mult)
                    ended(op)
                    bias = w[{"gat": "b2", "mid": "b3a", "last": "b3b"}[kind] + "_all"]
                    for j in js:
                        op = v.tensor_tensor(pre[:, j, :], pre[:, j, :], bias[:, :], ALU.add)
                    if kind == "gat":
                        ended(op)
                        v.wait_ge(x_in.h, x_in.at(i))
                        op = v.tensor_tensor(pre, pre, xin, ALU.add)
                    ended(op)
                if kind == "gru":
                    for j in js:
                        v.tensor_copy(small[:, j, 0:NREL], one(acc[:, block_of(j), D:D + NREL]))
                        v.tensor_copy(pre[:, j, :], one(acc[:, block_of(j), 0:D])).then_inc(red_copied.h, 1)
                    for j in js:
                        v.wait_ge(gates.h, gates.at(i * BATCH + j))
                        v.tensor_tensor(pre[:, j, :], rg[:, j, :], ps[:, 5 + j % 2, D:2 * D], ALU.mult).then_inc(gru_a.h, 1)
                        v.wait_ge(gru_a.h, gru_a.at(i * BATCH + j))
                        v.tensor_tensor(pre[:, j, :], pre[:, j, :], ps[:, 5 + j % 2, 0:D], ALU.add).then_inc(arg.h, 1)
                    v.wait_ge(tanh.h, tanh.at(i * BATCH + BATCH - 1))
                    v.wait_ge(x_in.h, x_in.at(i))
                    ended(v.tensor_tensor(rg, xin, pre, ALU.subtract))
                    ended(v.tensor_tensor(rg, rg, zg, ALU.mult))
                    ended(v.tensor_tensor(rg, rg, pre, ALU.add))
                v.wait_ge(stored.h, stored.at(i - 1))
                if kind == "sage":
                    v.wait_ge(x_in.h, x_in.at(i))
                    for j in js:
                        v.wait_ge(products.h, products.at(i * BATCH + j))
                        op = v.tensor_tensor(y[:, j, :], ps[:, 3 + j % 2, 0:D], xin[:, j, :], ALU.add)
                        op.then_inc(used_in.h, 1)
                    v.wait_ge(used_in.h, used_in.at(i * BATCH + BATCH - 1))
                elif kind == "gru":
                    ended(v.tensor_tensor(y, rg, xin, ALU.add))
                elif kind == "mid":
                    for j in js:
                        v.tensor_scalar(y[:, j, :], pre[:, j, :], 0.0, None, ALU.max).then_inc(x_new.h, 1)
                else:
                    if kind == "last":
                        v.wait_ge(x_in.h, x_in.at(i))
                    ended(v.scalar_tensor_tensor(out=y, in0=pre, scalar=0.0, in1=xin, op0=ALU.max, op1=ALU.add))
                if norm:
                    for j in js:
                        op = v.bn_stats(stats[:, j, :], y[:, j, :])
                    op.then_inc(norm_step.h, 1)
                    v.wait_ge(norm_step.h, norm_step.at(i, 1))
                    settle(v, V)
                    for j in js:
                        op = v.bn_aggr(mv[:, j, :], stats[:, j, :])
                    op.then_inc(norm_step.h, 1)
                    v.wait_ge(norm_step.h, norm_step.at(i, 2))
                    v.tensor_scalar(mv[:, :, 1:2], mv[:, :, 1:2], EPS, None, ALU.add).then_inc(norm_step.h, 1)
                    v.wait_ge(rstd.h, rstd.at(i))
                    v.reciprocal(mv[:, :, 1:2], mv[:, :, 1:2]).then_inc(norm_step.h, 1)
                    v.wait_ge(norm_step.h, norm_step.at(i, 4))
                    for j in js:
                        v.tensor_scalar(y[:, j, :], y[:, j, :], mv[:, j, 0:1], mv[:, j, 1:2], ALU.subtract, ALU.mult).then_inc(x_new.h, 1)
                v.engine_nop().then_inc(dve_step.h, 8 - step[0])

        @block.scalar
        def _(act):
            with act.Fori(0, NBATCH) as i:
                js = range(BATCH)
                if kind == "gru":
                    for j in js:
                        act.wait_ge(c_turned.h, c_turned.at(i * BATCH + j))
                        act.copy(ct[0:NREL, j, :], ps[0:NREL, (2, 7)[j % 2], 0:P]).then_inc(c_copied.h, 1)
                if project:
                    for j in js:
                        act.wait_ge(turned_in.h, turned_in.at(i * BATCH + j))
                        act.copy(tin[:, j, :], ps[:, j % 2, :]).then_inc(copied_in.h, 1)
                if kind == "gru":
                    for j in js:
                        act.wait_ge(products.h, products.at(i * BATCH + j))
                        act.activation(rg[:, j, :], ps[:, 3 + j % 2, 0:D], ACT.Sigmoid)
                        act.activation(zg[:, j, :], ps[:, 3 + j % 2, D:2 * D], ACT.Sigmoid).then_inc(gates.h, 1)
                    act.wait_ge(arg.h, arg.at(i * BATCH + BATCH - 1))
                    for j in js:
                        act.activation(pre[:, j, :], pre[:, j, :], ACT.Tanh).then_inc(tanh.h, 1)
                if norm:
                    act.wait_ge(norm_step.h, norm_step.at(i, 3))
                    act.activation(mv[:, :, 1:2], mv[:, :, 1:2], ACT.Sqrt).then_inc(rstd.h, 1)
                if table:
                    for j in js:
                        act.wait_ge(turned_out.h, turned_out.at(i * BATCH + j))
                        act.copy(tin[:, j, 0:D], ps[:, j % 2, 0:D]).then_inc(copied_out.h, 1)
                    act.wait_ge(stored.h, stored.at(i - 1))
                    act.wait_ge(V["cleared"].h, V["cleared"].at(0, 1))
                    for j in js:
                        act.wait_ge(table_mm.h, table_mm.at(i * BATCH + j))
                        got = ps[:, 3 + j % 2, :]
                        act.copy(heads(tab[:, j, 0:FW])[:, :, 0:HD], heads(got[:, 0:FW])[:, :, 0:HD])
                        act.copy(tab[:, j, FW:ROW], got[:, FW:ROW])
                        act.copy(er_sb[:, bass.ds((i * BATCH + j) * H, H)], got[:, ROW:ROW + H]).then_inc(table_copied.h, 1)

        @block.tensor
        def _(te):
            with te.Fori(0, NBATCH) as i:
                js = range(BATCH)

                if kind == "gru":
                    te.wait_ge(c_copied.h, c_copied.at(i * BATCH - 1))
                    for j in js:
                        if j >= 2:
                            te.wait_ge(c_copied.h, c_copied.at(i * BATCH + j - 2))
                        te.wait_ge(red_copied.h, red_copied.at(i * BATCH + j))
                        te.transpose(ps[0:NREL, (2, 7)[j % 2], 0:P], small[:, j, 0:NREL], ident[:, :]).then_inc(c_turned.h, 1)
                if project:
                    te.wait_ge(x_in.h, x_in.at(i))
                    last = copied_out if table else copied_in
                    te.wait_ge(last.h, last.at(i * BATCH - 1))
                    for j in js:
                        if j >= 2:
                            te.wait_ge(copied_in.h, copied_in.at(i * BATCH + j - 2))
                        if kind == "sage":
                            te.wait_ge(arg.h, arg.at(i * BATCH + j))
                        else:
                            te.wait_ge(c_copied.h, c_copied.at(i * BATCH + j))
                        for c in range(2):
                            to = ps[:, j % 2, c * P:(c + 1) * P]
                            if kind == "sage":
                                te.transpose(to, pre[:, j, c * P:(c + 1) * P], ident[:, :])
                            else:
                                te.matmul(to, pre[:, j, c * P:(c + 1) * P], ident[:, :], start=True, stop=False)
                                te.matmul(to, w["rel"][:, c * P:(c + 1) * P], ct[0:NREL, j, :], start=False, stop=True)
                        for c in range(2):
                            mm = te.transpose(ps[:, j % 2, (2 + c) * P:(3 + c) * P], xin[:, j, c * P:(c + 1) * P], ident[:, :])
                        mm.then_inc(turned_in.h, 1)
                    if table:
                        te.wait_ge(table_copied.h, table_copied.at(i * BATCH - 1))
                    for j in js:
                        te.wait_ge(copied_in.h, copied_in.at(i * BATCH + j))
                        n = i * BATCH + j
                        if kind == "sage":
                            te.wait_ge(used_in.h, used_in.at(n - 2))
                            for c in range(2):
                                te.matmul(ps[:, 3 + j % 2, 0:D], tin[:, j, c * P:(c + 1) * P], w["wn"][:, c, :], start=(c == 0), stop=False)
                            for c in range(2):
                                te.matmul(ps[:, 3 + j % 2, 0:D], tin[:, j, (2 + c) * P:(3 + c) * P], w["ws"][:, c, :], start=False, stop=False)
                            te.matmul(ps[:, 3 + j % 2, 0:D], ones[0:1, :], w["b0"][:, :], start=False, stop=True).then_inc(products.h, 1)
                        else:
                            te.wait_ge(gates.h, gates.at(n - 2))
                            te.wait_ge(arg.h, arg.at(n - 2))
                            rz, hn, inn = ps[:, 3 + j % 2, :], ps[:, 5 + j % 2, D:2 * D], ps[:, 5 + j % 2, 0:D]
                            for c in range(2):
                                te.matmul(rz, tin[:, j, c * P:(c + 1) * P], w["wih"][:, c, 0:2 * D], start=(c == 0), stop=False)
                            for c in range(2):
                                te.matmul(rz, tin[:, j, (2 + c) * P:(3 + c) * P], w["whh"][:, c, 0:2 * D], start=False, stop=False)
                            te.matmul(rz, ones[0:1, :], w["brz"][:, :], start=False, stop=True)
                            for to, at, ww, b in ((inn, 0, w["wih"], w["bih"]), (hn, 2, w["whh"], w["bhh"])):
                                for c in range(2):
                                    te.matmul(to, tin[:, j, (at + c) * P:(at + c + 1) * P], ww[:, c, 2 * D:], start=(c == 0), stop=False)
                                mm = te.matmul(to, ones[0:1, :], b[:, 2 * D:], start=False, stop=True)
                            mm.then_inc(products.h, 1)
                if table:
                    if project:
                        te.wait_ge(copied_in.h, copied_in.at(i * BATCH + BATCH - 1))
                    for j in js:
                        te.wait_ge(x_new.h, x_new.at(i * BATCH + j))
                        te.wait_ge(copied_out.h, copied_out.at(i * BATCH + j - 2))
                        for c in range(2):
                            mm = te.transpose(ps[:, j % 2, c * P:(c + 1) * P], y[:, j, c * P:(c + 1) * P], ident[:, :])
                        mm.then_inc(turned_out.h, 1)
                    if kind == "gru":
                        te.wait_ge(gates.h, gates.at(i * BATCH + BATCH - 1))
                    for j in js:
                        te.wait_ge(copied_out.h, copied_out.at(i * BATCH + j))
                        te.wait_ge(table_copied.h, table_copied.at(i * BATCH + j - 2))
                        for c in range(2):
                            mm = te.matmul(ps[:, 3 + j % 2, 0:FW + 2 * H], tin[:, j, c * P:(c + 1) * P], wt[:, c, :], start=(c == 0), stop=(c == 1))
                        mm.then_inc(table_mm.h, 1)

    dve_step.phase_ended(NBATCH)
    stored.phase_ended(NBATCH)
    if need_x:
        x_in.phase_ended(NBATCH)
    if out_dram is not None:
        store_x.phase_ended(NBATCH)
    x_new.phase_ended(BLOCKS)
    if norm:
        norm_step.phase_ended(NBATCH)
        rstd.phase_ended(NBATCH)
    if project:
        for c in (turned_in, copied_in, products, arg):
            c.phase_ended(BLOCKS)
        if kind == "sage":
            used_in.phase_ended(BLOCKS)
    if kind == "gru":
        for c in (c_turned, c_copied, gates, tanh, gru_a, red_copied):
            c.phase_ended(BLOCKS)
    if table:
        V["cleared"].base += 1
        store_t.phase_ended(NBATCH)
        for c in (turned_out, copied_out, table_mm, table_copied):
            c.phase_ended(BLOCKS)


_OUT_ROWS = NPAD


def kernel(**inputs):
    import numpy as np
    import concourse.bacc as bacc
    from concourse.bass_utils import run_bass_kernel_spmd as launch

    def arr(name):
        return np.ascontiguousarray(inputs[name])

    def padded(x, rows, fill):
        out = np.full((rows,) + x.shape[1:], fill, x.dtype)
        out[:x.shape[0]] = x
        return out

    edges = TROWS * P
    dst = padded(arr("dst"), edges, NPAD)
    feat = {"x": padded(arr("x"), NPAD, 0),
            "src": padded(arr("src"), edges, 0).reshape(TROWS, P),
            "dst": dst.reshape(TROWS, P),
            "etype": padded(arr("edge_type_16"), edges, 0).reshape(TROWS, P),
            "dlast": np.ascontiguousarray(dst[P - 1:TILES * P:P]),
            "edge": np.ascontiguousarray(padded(arr("edge_attr_256"), edges, 0).reshape(TROWS, P, 2, P).transpose(0, 3, 2, 1)).reshape(TROWS, P, D)}
    feat["ws"], feat["wn"], feat["b0"] = arr("L0_gnn_W_self"), arr("L0_gnn_W_neigh"), arr("L0_gnn_b")
    feat["rel"], feat["bih"], feat["bhh"] = arr("L1_gnn_relvectors"), arr("L1_gnn_b_ih"), arr("L1_gnn_b_hh")
    feat["wih"], feat["whh"] = (np.ascontiguousarray(arr(n).T) for n in ("L1_gnn_w_ih", "L1_gnn_w_hh"))
    for name, x in (("w2", arr("L2_gnn_W").T), ("we", arr("L2_gnn_We").T), ("w3a", arr("L3_gnn_W1")), ("w3b", arr("L3_gnn_W2"))):
        feat[name], feat[name + "_t"] = np.ascontiguousarray(x), np.ascontiguousarray(x.T)
    for name, x in (("al2", "L2_gnn_attn_l"), ("ar2", "L2_gnn_attn_r"), ("ae2", "L2_gnn_attn_e"), ("al3a", "L3_gnn_al1"),
                    ("ar3a", "L3_gnn_ar1"), ("al3b", "L3_gnn_al2"), ("ar3b", "L3_gnn_ar2")):
        feat[name] = arr(x).reshape(-1)
    feat["bias2"], feat["bias3a"], feat["bias3b"] = arr("L2_gnn_bias"), arr("L3_gnn_b1"), arr("L3_gnn_b2")
    feat["b2"], feat["b3a"], feat["b3b"] = feat.pop("bias2"), feat.pop("bias3a"), feat.pop("bias3b")
    feat["ident"] = np.eye(P, dtype=np.float32)
    feat["kio"] = np.arange(KPAD, dtype=np.float32)
    feat["kcol"] = np.ascontiguousarray(np.arange(KPAD, dtype=np.float32).reshape(CHUNKS, P).T)
    feat["pcol"] = np.arange(P, dtype=np.float32).reshape(P, 1)
    feat["headmask"] = np.kron(np.eye(H, dtype=np.float32), np.ones((HD, 1), np.float32))

    nc = bacc.Bacc("TRN2", target_bir_lowering=False, num_devices=1)
    aps, sent = {}, {}
    for name, x in feat.items():
        sent[f"in_{name}"] = x
        aps[name] = nc.dram_tensor(f"in_{name}", x.shape, mybir.dt.from_np(x.dtype), kind="ExternalInput").ap()
    aps["out"] = nc.dram_tensor("out_0", (NPAD, D), F32, kind="ExternalOutput").ap()
    build(nc, aps)
    r = launch(nc, [sent], core_ids=[0])
    return r.results[0]["out_0"][:N]
```

```python
from contextlib import ExitStack

import concourse.bass as bass
from concourse import mybir

F32 = mybir.dt.float32
I32 = mybir.dt.int32
BF16 = mybir.dt.bfloat16
ALU = mybir.AluOpType
ACT = mybir.ActivationFunctionType
ENG = mybir.EngineType

P = 128
N = 6250
E = 106250
D = 256
H = 8
HD = D // H
NREL = 16
BLOCKS = -(-N // P)
TILES = -(-E // P)
G = 8
SLOTS = 3
GROUPS = -(-(TILES + BLOCKS - 1) // (G * SLOTS)) * SLOTS
LOOPS = GROUPS // SLOTS
CHUNKS = -(-(GROUPS + SLOTS) * G // P)
KPAD = CHUNKS * P
GE = G * P
NPAD = BLOCKS * P
TROWS = TILES + 1
HW = HD + 1
FW = H * HW
ROW = FW + H
BATCH = 7
NBATCH = BLOCKS // BATCH
BIG = 1.0e30
EPS = 1e-5
SLOPE = 0.2
HALF = G // 2
RECORD = 8
FAR = 2 * HALF
ONE_TURN = {t: FAR + HALF - t for t in range(1, HALF)}
FARTHER = 2 * FAR
assert BLOCKS % BATCH == 0 and (GROUPS + SLOTS) * G <= KPAD


class Count:

    def __init__(self, handle, per, credit):
        self.h, self.per, self.base = handle, per, per * credit

    def at(self, unit, part=None):
        return unit * self.per + (self.base + (self.per if part is None else part))

    def phase_ended(self, units):
        self.base += self.per * units


def build(nc, a):
    ctx = ExitStack()
    with ctx:
        def sb(name, shape, dt=F32):
            return ctx.enter_context(nc.sbuf_tensor(name, shape, dt))

        def sem(name):
            return ctx.enter_context(nc.semaphore(name))

        ps = ctx.enter_context(nc.psum_tensor("ps", [P, 8, 512], F32))

        md_lin = nc.dram_tensor("md_lin", [KPAD * P + 1], F32, kind="Internal").ap()
        md_dram = nc.dram_tensor("md_dram", [KPAD * P], BF16, kind="Internal").ap()
        rst_dram = nc.dram_tensor("rst_dram", [KPAD * P], F32, kind="Internal").ap()
        x1_dram = nc.dram_tensor("x1_dram", [NPAD, D], F32, kind="Internal").ap()
        x2_dram = nc.dram_tensor("x2_dram", [NPAD, D], F32, kind="Internal").ap()
        x3_dram = nc.dram_tensor("x3_dram", [NPAD, D], F32, kind="Internal").ap()
        tab_dram = [nc.dram_tensor(f"tab{n}_dram", [NPAD, ROW], F32, kind="Internal").ap() for n in range(3)]

        ident = sb("ident", [P, P])
        iota = sb("iota", [P, P])
        iota_neg = sb("iota_neg", [P, 1])
        ones = sb("ones", [P, P])
        src_t = sb("src_t", [P, KPAD], I32)
        md_t = sb("md_t", [P, KPAD])
        blk_row = sb("blk_row", [1, G + KPAD], I32)
        tile_row = sb("tile_row", [1, KPAD], I32)
        record = sb("record", [1, KPAD // G, RECORD], I32)
        open_md = sb("open_md", [H, GROUPS + 1])

        acc = sb("acc", [P, BLOCKS, ROW])
        er_sb = sb("er_sb", [P, BLOCKS, H])
        er_parts = sb("er_parts", [P, BLOCKS, 3, H], BF16)
        er_rest = sb("er_rest", [P, BLOCKS, H])

        rows = sb("rows", [P, SLOTS, G, ROW])
        idx = sb("idx", [P, SLOTS, G], I32)
        hot = sb("hot", [P, SLOTS, G, P])

        def per_group(name, per):
            return Count(sem(name), per, SLOTS)

        def per_block(name, per=1):
            return Count(sem(name), per, BATCH)

        cleared = Count(sem("cleared"), 2, 0)
        settled = sem("settled")
        idx_ready = per_group("idx_ready", 1)
        gathered = [Count(sem(f"gathered{u}"), 16 * G, 0) for u in range(SLOTS)]
        hot_ready = per_group("hot_ready", 1)
        agg_ready = per_group("agg_ready", G)
        acc_done = per_group("acc_done", G)
        types_hot = per_group("types_hot", 1)
        resets = [Count(sem(f"resets{u}"), 16, 0) for u in range(SLOTS)]
        md_in = [Count(sem(f"md_in{u}"), 16, 0) for u in range(SLOTS)]
        edge_in = [Count(sem(f"edge_in{u}"), 16 * G, 0) for u in range(SLOTS)]
        turned_a = per_group("turned_a", 1)
        turned_ready = per_group("turned_ready", 1)
        er_ready = per_group("er_ready", 1)
        er_summed = per_group("er_summed", 1)
        hot_a = per_group("hot_a", 1)
        fe_ready = per_group("fe_ready", G)
        fe_added = per_group("fe_added", G)
        score_a = per_group("score_a", 1)
        score_b = per_group("score_b", 1)
        score_turned = per_group("score_turned", 1)
        scan_a = per_group("scan_a", 1)
        scan_b = per_group("scan_b", 1)
        drop_ready = per_group("drop_ready", 1)
        drop_a = per_group("drop_a", 2)
        ref_turned = per_group("ref_turned", 1)
        drop_mm = per_group("drop_mm", 1)
        shifted = per_group("shifted", 1)
        weight_ready = per_group("weight_ready", 1)
        scale_ready = per_group("scale_ready", 1)
        msg_ready = per_group("msg_ready", 2)
        rescaled = per_group("rescaled", 1)
        credited = [er_summed, hot_a, idx_ready, hot_ready, agg_ready, acc_done, types_hot, turned_a, turned_ready, er_ready,
                    fe_ready, fe_added, score_a, score_b, score_turned, scan_a, scan_b, drop_a, drop_ready,
                    ref_turned, drop_mm, shifted, weight_ready, scale_ready, msg_ready, rescaled]
        x_in = Count(sem("x_in"), 16, 0)
        c_turned, c_copied, turned_in, copied_in, products, gates, arg, tanh, used_in, x_new, turned_out, copied_out, \
            table_mm, table_copied = (per_block(n) for n in (
                "c_turned", "c_copied", "turned_in", "copied_in", "products", "gates", "arg", "tanh", "used_in", "x_new",
                "turned_out", "copied_out", "table_mm", "table_copied"))
        gru_a, red_copied = per_block("gru_a"), per_block("red_copied")
        dve_step = Count(sem("dve_step"), 8, 1)
        norm_step = Count(sem("norm_step"), 4, 1)
        rstd = Count(sem("rstd"), 1, 1)
        stored = Count(sem("stored"), 1, 1)
        credited += [c_turned, c_copied, turned_in, copied_in, products, gates, arg, tanh, used_in, x_new, turned_out,
                     copied_out, table_mm, table_copied, dve_step, stored, gru_a, red_copied, norm_step, rstd]
        store_x = Count(sem("store_x"), 16, 0)
        store_t = Count(sem("store_t"), 16, 0)

        edge_t = sb("edge_t", [P, SLOTS, G, D])
        nsmall = sb("nsmall", [P, BATCH, 2 * H])
        wts = {name: sb(name, [P, 2, FW + 2 * H]) for name in ("w2", "we", "w3a", "w3b")}
        for name in ("b2", "b3a", "b3b"):
            wts[name + "_all"] = sb(name + "_all", [P, D])
        early = ctx.enter_context(ExitStack())

        def sb_early(name, shape):
            return early.enter_context(nc.sbuf_tensor(name, shape, F32))

        type_t = sb_early("type_t", [P, KPAD])
        load_weights(nc, a, wts, sb_early, sem, ps, ones, credited)
        prep(nc, a, sb, sem, ps, dict(src_t=src_t, md_t=md_t, type_t=type_t, blk_row=blk_row, tile_row=tile_row, record=record,
                                     open_md=open_md, ident=ident, iota=iota, iota_neg=iota_neg, ones=ones, md_lin=md_lin,
                                     rst_dram=rst_dram, md_dram=md_dram, acc=acc, rows=rows))

        V = dict(locals())
        sum_phase(nc, a, V, a["x"], None)
        node_phase(nc, a, V, "sage", a["x"], x1_dram, None, wts)
        sum_phase(nc, a, V, x1_dram, type_t)
        node_phase(nc, a, V, "gru", x1_dram, x2_dram, (tab_dram[0], wts["w2"]), wts)
        early.close()

        V["turned"] = sb("turned", [P, GE], BF16)
        V["md_all"] = sb("md_all", [P, SLOTS, GE], BF16)
        V["off"] = sb("off", [P, GE], BF16)
        V["off_hot"] = sb("off_hot", [P, G, P], BF16)
        V["score_er"] = sb("score_er", [P, G, H])
        for name in ("score", "score_raw", "shift", "weight"):
            V[name] = sb(name, [P, SLOTS, G, H])
        V["rst_sb"] = sb("rst_sb", [H, SLOTS, GE + 1])
        V["run"] = sb("run", [H, GE])
        V["ref"] = sb("ref", [H, GE])
        V["carry"] = sb("carry", [H, SLOTS])
        V["drop"] = sb("drop", [H, SLOTS, H])
        V["dropc"] = sb("dropc", [H, SLOTS])
        V["openhot"] = sb("openhot", [H, SLOTS, P])
        V["scale"] = sb("scale", [P, SLOTS, H])
        gat_phase(nc, a, V, tab_dram[0], wts["we"])
        node_phase(nc, a, V, "gat", x2_dram, x3_dram, (tab_dram[1], wts["w3a"]), wts)
        gat_phase(nc, a, V, tab_dram[1], None)
        node_phase(nc, a, V, "mid", None, None, (tab_dram[2], wts["w3b"]), wts)
        gat_phase(nc, a, V, tab_dram[2], None)
        node_phase(nc, a, V, "last", x3_dram, a["out"], None, wts)


def prep(nc, a, sb, sem, ps, V):
    ident, iota, ones = V["ident"], V["iota"], V["ones"]
    md_lin, rst_dram = V["md_lin"], V["rst_dram"]
    with ExitStack() as tmp:
        def t(name, shape, dt=F32):
            return tmp.enter_context(nc.sbuf_tensor(name, shape, dt))

        last_i = t("last_i", [BLOCKS, TILES], I32)
        last_f = t("last_f", [BLOCKS, TILES])
        nblk = t("nblk", [P, 1])
        bound = t("bound", [P, 1])
        before = t("before", [BLOCKS, 1])
        turn_at = t("turn_at", [BLOCKS, 1])
        kio = t("kio", [P, KPAD])
        bcol = t("bcol", [P, CHUNKS])
        kcol = t("kcol", [P, CHUNKS])
        tcol_f = t("tcol_f", [P, CHUNKS])
        tcol = t("tcol", [P, CHUNKS], I32)
        row_i = V["rows"][:, :, :, :].rearrange("p a b c -> p (a b c)")[:, 0:3 * KPAD].bitcast(I32).rearrange("p (n c e) -> p n c e", n=3, e=P)
        room = V["acc"][:, :, :].rearrange("p b w -> p (b w)")

        past = room[0:BLOCKS, 9 * KPAD:10 * KPAD]
        units = KPAD // G - 1
        spans = room[0:1, 10 * KPAD:10 * KPAD + 2 * HALF * units].rearrange("a (g n k) -> a g n k", n=2, k=HALF)
        turned_far, span_sums = (room[0:1, n * KPAD:n * KPAD + 2 * units].rearrange("a (g n) -> a g n", n=2) for n in (11, 12))

        def lent(n, count=1):
            return room[:, n * KPAD:(n + count) * KPAD].rearrange("p (c e) -> p c e", e=P)

        row_f = lent(0, 3).rearrange("p (n c) e -> p n c e", n=3)
        rel, m1, md, before_md = (lent(n) for n in range(3, 7))
        pad = t("pad", [1, 2])
        md_b = t("md_b", [P, CHUNKS, P], BF16)
        op = t("op", [H, 2, GROUPS + 1])
        brow_f, trow_f = (room[0:1, n * KPAD:(n + 1) * KPAD] for n in (7, 8))
        ld, io, vv, pe, g_in, st, l2, st2, l3 = (sem(f"prep_{n}") for n in
                                                 ("load", "iota", "vec", "pe", "gather", "store", "shifted", "rst", "open"))
        with nc.Block() as block:
            @block.sync
            def _(sp):
                sp.dma_start(last_i[:, :], a["dlast"].rearrange("(a n) -> a n", a=1).to_broadcast([BLOCKS, TILES])).then_inc(ld, 16)
                sp.dma_start(ident[:, :], a["ident"]).then_inc(ld, 16)
                sp.dma_start(kio[:, :], a["kio"].rearrange("(a n) -> a n", a=1).to_broadcast([P, KPAD])).then_inc(ld, 16)
                sp.dma_start(kcol[:, :], a["kcol"]).then_inc(ld, 16)
                sp.dma_start(nblk[:, :], a["pcol"]).then_inc(ld, 16)
                sp.wait_ge(vv, 10)
                with nc.allow_non_contiguous_dma(reason="pads"):
                    sp.dma_start(md_lin[1:1 + KPAD * P].rearrange("(c p e) -> p c e", c=CHUNKS, e=P), md[:, :, :]).then_inc(st, 16)
                    sp.dma_start(md_lin[0:1].rearrange("(a n) -> a n", a=1), pad[0:1, 0:1]).then_inc(st, 16)
                    sp.wait_ge(st, 32)
                    sp.dma_start(before_md[:, :, :], md_lin[0:KPAD * P].rearrange("(c p e) -> p c e", c=CHUNKS, e=P)).then_inc(l2, 16)
                    for n in range(2):
                        first = md_lin[1 - n:1 - n + (GROUPS + 1) * GE].rearrange("(g e) -> g e", e=GE)[:, 0:1]
                        sp.dma_start(op[:, n, :], first.rearrange("g a -> a g").to_broadcast([H, GROUPS + 1])).then_inc(l3, 16)
                    sp.wait_ge(vv, 12)
                    sp.dma_start(V["md_dram"].rearrange("(c p e) -> p c e", c=CHUNKS, e=P), md_b[:, :, :]).then_inc(st2, 16)
                    sp.dma_start(rst_dram.rearrange("(c p e) -> p c e", c=CHUNKS, e=P), before_md[:, :, :]).then_inc(st2, 16)
                    sp.wait_ge(st2, 32)

            @block.gpsimd
            def _(pool):
                pool.wait_ge(vv, 7)
                for n, tab in enumerate((a["src"], a["dst"], a["etype"])):
                    for c in range(CHUNKS):
                        pool.indirect_dma_start(out=row_i[:, n, c, :], out_offset=None, in_=tab,
                                                in_offset=bass.IndirectOffsetOnAxis(ap=tcol[:, c:c + 1], axis=0)).then_inc(g_in, 16)
                pool.wait_ge(g_in, 16 * 3 * CHUNKS)

            @block.tensor
            def _(te):
                te.wait_ge(vv, 4)
                half = KPAD // 2
                for n in range(2):
                    te.matmul(ps[0:1, n, 0:half], ones[0:BLOCKS - 1, 0:1], past[0:BLOCKS - 1, n * half:(n + 1) * half], start=True, stop=True)
                for c in range(CHUNKS):
                    mm = te.matmul(ps[:, 2, c:c + 1], past[0:BLOCKS - 1, c * P:(c + 1) * P], ones[0:BLOCKS - 1, 0:1], start=True, stop=True)
                mm.then_inc(pe, 1)
                te.wait_ge(vv, 10)
                for n in range(3):
                    src = (row_f[:, 0], md, row_f[:, 2])[n]
                    for c in range(CHUNKS):
                        bank, at = 3 + (n * CHUNKS + c) // 4 % 5, (n * CHUNKS + c) % 4
                        if n * CHUNKS + c == 20:
                            te.wait_ge(vv, 14)
                        te.transpose(ps[:, bank, at * P:(at + 1) * P], src[:, c, :], ident[:, :]).then_inc(pe, 1)

            @block.vector
            def _(v):
                v.memset(ones[:, :], 1.0)
                v.memset(pad[:, :], -7.0)
                v.memset(V["record"][:, :, :], 0)
                v.wait_ge(ld, 16 * 5)
                v.tensor_copy(iota[:, :], kio[:, 0:P])
                v.tensor_scalar(V["iota_neg"][:, :], nblk[:, :], -1.0, None, ALU.mult)
                v.tensor_scalar(bound[:, :], nblk[:, :], float(P), float(P), ALU.mult, ALU.add).then_inc(vv, 1)
                v.tensor_copy(last_f[:, :], last_i[:, :]).then_inc(vv, 1)
                v.wait_ge(vv, 2)
                v.tensor_scalar(last_f[:, :], last_f[:, :], bound[0:BLOCKS, 0:1], None, ALU.is_lt).then_inc(vv, 1)
                v.wait_ge(vv, 3)
                v.reduce_sum(before[:, :], last_f[:, :], mybir.AxisListType.X).then_inc(io, 1)
                v.wait_ge(io, 1)
                v.tensor_scalar(turn_at[:, :], before[:, :], nblk[0:BLOCKS, 0:1], 1.0, ALU.add, ALU.add).then_inc(io, 1)
                v.wait_ge(io, 2)
                v.tensor_scalar(past[:, :], kio[0:BLOCKS, :], turn_at[:, 0:1], None, ALU.is_ge).then_inc(vv, 1)
                v.wait_ge(pe, 1)
                v.tensor_copy(bcol[:, :], ps[:, 2, 0:CHUNKS]).then_inc(vv, 1)
                half = KPAD // 2
                for n in range(2):
                    v.tensor_copy(brow_f[:, n * half:(n + 1) * half], ps[0:1, n, 0:half])
                v.tensor_tensor(tcol_f[:, :], kcol[:, :], ps[:, 2, 0:CHUNKS], ALU.subtract).then_inc(vv, 1)
                v.wait_ge(vv, 6)
                v.tensor_scalar(tcol[:, :], tcol_f[:, :], float(TILES), None, ALU.min).then_inc(vv, 1)
                v.tensor_tensor(trow_f[:, :], kio[0:1, :], brow_f[:, :], ALU.subtract).then_inc(io, 1)
                v.memset(V["blk_row"][:, 0:G], 0)
                v.tensor_copy(V["blk_row"][:, G:], brow_f[:, :])
                groups = brow_f[:, :].rearrange("a (g k) -> a g k", k=G)
                v.wait_ge(io, 3)
                for n in range(2):
                    v.tensor_copy(V["record"][:, 1:, n:n + 1], groups[:, :-1, n * HALF:n * HALF + 1])
                    v.tensor_copy(V["record"][:, 1:, 5 + n:6 + n], groups[:, :-1, (n + 1) * HALF - 1:(n + 1) * HALF])
                    first = groups[:, :-1, n * HALF:n * HALF + 1]
                    v.tensor_tensor(spans[:, :, n, :], groups[:, :-1, n * HALF:(n + 1) * HALF], first.to_broadcast([1, KPAD // G - 1, HALF]), ALU.subtract)
                    v.tensor_tensor(turned_far[:, :, n], groups[:, :-1, (n + 1) * HALF - 1:(n + 1) * HALF].rearrange("a g k -> a (g k)"), first.rearrange("a g k -> a (g k)"), ALU.subtract).then_inc(io, 1)
                v.wait_ge(io, 5)
                v.tensor_reduce(span_sums[:, :, :], spans[:, :, :, :], mybir.AxisListType.X, ALU.add).then_inc(io, 1)
                v.wait_ge(io, 6)
                v.scalar_tensor_tensor(out=V["record"][:, 1:, 2:4], in0=turned_far[:, :, :], scalar=float(FAR), in1=span_sums[:, :, :], op0=ALU.mult, op1=ALU.add)
                v.tensor_copy(V["record"][:, :, 4:5], groups[:, :, 0:1])
                v.tensor_scalar(V["tile_row"][:, :], trow_f[:, :], float(TILES), None, ALU.min)
                v.wait_ge(g_in, 16 * 3 * CHUNKS)
                v.tensor_copy(row_f[:, :, :, :], row_i[:, :, :, :]).then_inc(vv, 1)
                v.tensor_scalar(bcol[:, :], bcol[:, :], float(P), None, ALU.mult).then_inc(io, 1)
                v.wait_ge(vv, 8)
                v.wait_ge(io, 7)
                for c in range(CHUNKS):
                    v.tensor_scalar(rel[:, c, :], row_f[:, 1, c, :], bcol[:, c:c + 1], None, ALU.subtract).then_inc(io, 1)
                v.wait_ge(io, 7 + CHUNKS)
                v.tensor_scalar(m1[:, :, :], rel[:, :, :], 0.0, None, ALU.is_ge).then_inc(io, 1)
                v.wait_ge(io, 8 + CHUNKS)
                v.scalar_tensor_tensor(out=m1[:, :, :], in0=rel[:, :, :], scalar=float(P - 1), in1=m1[:, :, :], op0=ALU.is_le, op1=ALU.mult).then_inc(vv, 1)
                v.wait_ge(vv, 9)
                v.scalar_tensor_tensor(out=md[:, :, :], in0=rel[:, :, :], scalar=1.0, in1=m1[:, :, :], op0=ALU.add, op1=ALU.mult).then_inc(io, 1)
                v.wait_ge(io, 9 + CHUNKS)
                v.tensor_scalar(md[:, :, :], md[:, :, :], -1.0, None, ALU.add).then_inc(vv, 1)
                v.wait_ge(vv, 10)
                v.tensor_copy(md_b[:, :, :], md[:, :, :])
                v.wait_ge(l2, 16)
                v.tensor_tensor(before_md[:, :, :], before_md[:, :, :], md[:, :, :], ALU.not_equal).then_inc(vv, 1)
                v.wait_ge(vv, 11)
                v.tensor_scalar(before_md[:, :, :], before_md[:, :, :], -BIG, None, ALU.mult).then_inc(vv, 1)
                v.wait_ge(l3, 32)
                v.tensor_tensor(op[:, 1, :], op[:, 0, :], op[:, 1, :], ALU.is_equal).then_inc(io, 1)
                v.wait_ge(io, 10 + CHUNKS)
                v.scalar_tensor_tensor(out=V["open_md"][:, :], in0=op[:, 0, :], scalar=1.0, in1=op[:, 1, :], op0=ALU.add, op1=ALU.mult).then_inc(io, 1)
                v.wait_ge(io, 11 + CHUNKS)
                v.tensor_scalar(V["open_md"][:, :], V["open_md"][:, :], -1.0, None, ALU.add)
                outs = (V["src_t"], V["md_t"], V["type_t"])

                def turn_out(j):
                    n, c = j // CHUNKS, j % CHUNKS
                    return v.tensor_copy(outs[n][:, c * P:(c + 1) * P], ps[:, 3 + j // 4 % 5, j % 4 * P:(j % 4 + 1) * P])

                v.wait_ge(pe, 1 + 20)
                for j in range(20):
                    turn_out(j).then_inc(io, 1)
                v.wait_ge(io, 31 + CHUNKS)
                v.engine_nop().then_inc(vv, 2)
                v.wait_ge(pe, 1 + 3 * CHUNKS)
                for j in range(20, 3 * CHUNKS):
                    turn_out(j)


def load_weights(nc, a, w, sb, sem, ps, ones, credited):
    for name in ("ws", "wn"):
        w[name] = sb(name, [P, 2, D])
    for name in ("wih", "whh"):
        w[name] = sb(name, [P, 2, 3 * D])
    w["rel"] = sb("relv", [NREL, D])
    rowsb = {"b0": D, "bih": 3 * D, "bhh": 3 * D}
    for name, n in rowsb.items():
        w[name] = sb(name, [1, n])
    w["brz"] = sb("brz", [1, 2 * D])
    ld, on, pe, dv = (sem(f"weights_{n}") for n in ("load", "spread", "turned", "copied"))
    with ExitStack() as tmp:
        def t(name, shape):
            return tmp.enter_context(nc.sbuf_tensor(name, shape, F32))

        nat = {name: t(name + "_nat", [P, 2, D]) for name in ("w2", "we", "w3a", "w3b")}
        tr = {name: t(name + "_tr", [P, 2, D]) for name in ("w2", "we", "w3a", "w3b")}
        mask = t("headmask", [P, 2, H])
        cols = {"w2": ("al2", "ar2"), "we": ("ae2",), "w3a": ("al3a", "ar3a"), "w3b": ("al3b", "ar3b")}
        vec, spread = {}, {}
        for name, vs in cols.items():
            for x in vs:
                vec[x] = t(x + "_v", [P, 2])
                spread[x] = t(x + "_s", [P, 2, H])
        total = 0
        with nc.Block() as block:
            @block.sync
            def _(sp):
                nonlocal total
                loads = [(w[n][:, :, :], a[n].rearrange("(c p) n -> p c n", p=P)) for n in ("ws", "wn", "wih", "whh")]
                for n in nat:
                    loads.append((nat[n][:, :, :], a[n].rearrange("(c p) n -> p c n", p=P)))
                    loads.append((tr[n][:, :, :], a[n + "_t"].rearrange("(c p) n -> p c n", p=P)))
                loads.append((w["rel"][:, :], a["rel"]))
                loads += [(w[n][:, :], a[n].rearrange("(a n) -> a n", a=1)) for n in rowsb]
                loads += [(w[n + "_all"][:, :], a[n].rearrange("(a n) -> a n", a=1).to_broadcast([P, D])) for n in ("b2", "b3a", "b3b")]
                loads.append((mask[:, :, :], a["headmask"].rearrange("(c p) n -> p c n", p=P)))
                with nc.allow_non_contiguous_dma(reason="small vectors"):
                    loads += [(vec[x][:, :], a[x].rearrange("(c p) -> p c", p=P)) for x in vec]
                    for o, i in loads:
                        sp.dma_start(o, i).then_inc(ld, 16)
                total = 16 * len(loads)
                for c in credited:
                    sp.sem_inc(c.h, c.base)

            @block.vector
            def _(v):
                v.wait_ge(ld, total)
                for name in nat:
                    v.memset(w[name][:, :, :], 0.0).then_inc(dv, 1)
                v.wait_ge(dv, 4)
                for name in nat:
                    for c in range(2):
                        v.tensor_copy(w[name][:, c, 0:FW].rearrange("p (h d) -> p h d", h=H)[:, :, 0:HD],
                                      nat[name][:, c, :].rearrange("p (h d) -> p h d", h=H))
                v.tensor_tensor(w["brz"][:, :], w["bih"][:, 0:2 * D], w["bhh"][:, 0:2 * D], ALU.add)
                for x in vec:
                    for c in range(2):
                        v.tensor_scalar(spread[x][:, c, :], mask[:, c, :], vec[x][:, c:c + 1], None, ALU.mult).then_inc(on, 1)
                v.wait_ge(pe, 1)
                at = 0
                for name, vs in cols.items():
                    for j, x in enumerate(vs):
                        for c in range(2):
                            v.tensor_copy(w[name][:, c, FW + j * H:FW + (j + 1) * H], ps[:, 0, at:at + H])
                            at += H

            @block.tensor
            def _(te):
                te.wait_ge(on, 2 * len(vec))
                at = 0
                for name, vs in cols.items():
                    for x in vs:
                        for c in range(2):
                            for k in range(2):
                                mm = te.matmul(ps[:, 0, at:at + H], tr[name][:, k, c * P:(c + 1) * P], spread[x][:, k, :],
                                               start=(k == 0), stop=(k == 1))
                            at += H
                mm.then_inc(pe, 1)


def settle(eng, V):
    eng.sem_inc(V["settled"], 1)


def numbers_of(nc, engine, table, g, most):
    return numbers_at(nc, engine, table[0:1, bass.ds(g * G, G)], most)


def numbers_at(nc, engine, place, most):
    _, vals = nc.values_load_multi_w_load_instructions(
        place, engines=[engine], min_val=0, max_val=most,
        skip_runtime_bounds_check_because="the table's values are counts of at most BLOCKS - 1 turns, or a minimum with TILES")
    return vals


def gather_rows(nc, V, table, width, lag, extra):
    agg_ready, idx_ready = V["agg_ready"], V["idx_ready"]

    def body(pool):
        def group(g, u):
            pool.wait_ge(idx_ready.h, idx_ready.at(g))
            for k in range(G):
                if k % HALF == 0:
                    pool.wait_ge(agg_ready.h, agg_ready.at(g + lag - SLOTS, k + HALF))
                    settle(pool, V)
                pool.indirect_dma_start(out=V["rows"][:, u, k, 0:width], out_offset=None, in_=table,
                                        in_offset=bass.IndirectOffsetOnAxis(ap=V["idx"][:, u, k:k + 1], axis=0)
                                        ).then_inc(V["gathered"][u].h, 16)

        with pool.Fori(0, LOOPS) as i:
            for u in range(SLOTS):
                group(i * SLOTS + u, u)
        for g in range(GROUPS, GROUPS + extra):
            group(g, g % SLOTS)
    return body


def give_sources(act, V, g, u, after=None):
    if after is not None:
        act.wait_ge(V["gathered"][u].h, V["gathered"][u].at(after))
    act.copy(V["idx"][:, u, :], V["src_t"][:, bass.ds(g * G, G)]).then_inc(V["idx_ready"].h, 1)


def make_hot(v, V, g, u, lag=0):
    v.wait_ge(V["agg_ready"].h, V["agg_ready"].at(g + lag - SLOTS))
    for k in range(G):
        op = v.tensor_scalar(V["hot"][:, u, k, :], V["iota"][:, :], V["md_t"][:, bass.ds(g * G + k, 1)], None, ALU.is_equal)
    op.then_inc(V["hot_ready"].h, 1)


def sum_phase(nc, a, V, table, types):
    ps, rows, acc, hot = V["ps"], V["rows"], V["acc"], V["hot"]
    width = D + (NREL if types is not None else 1)
    hot_ready, agg_ready, acc_done, gathered, types_hot = (V[n] for n in ("hot_ready", "agg_ready", "acc_done", "gathered", "types_hot"))
    cleared, start = V["cleared"], 2 if types is None else 1
    with nc.Block() as block:
        block.gpsimd(gather_rows(nc, V, table, D, 0, 0))

        @block.scalar
        def _(act):
            for u in range(SLOTS):
                give_sources(act, V, u, u)
            with act.Fori(0, LOOPS) as i:
                for u in range(SLOTS):
                    give_sources(act, V, (i + 1) * SLOTS + u, u, i)

        @block.vector
        def _(v):
            v.memset(acc[:, :, :], 0.0).then_inc(cleared.h, 1)
            if types is None:
                v.memset(rows[:, :, :, D:D + 1], 1.0).then_inc(cleared.h, 1)
            v.wait_ge(cleared.h, cleared.at(0, start))
            make_hot(v, V, 0, 0)
            with v.Fori(0, LOOPS) as i:
                for u in range(SLOTS):
                    g = i * SLOTS + u
                    if types is not None:
                        for k in range(G):
                            op = v.tensor_scalar(rows[:, u, k, D:D + NREL], V["iota"][:, 0:NREL], types[:, bass.ds(g * G + k, 1)], None, ALU.is_equal)
                        op.then_inc(types_hot.h, 1)
                    make_hot(v, V, g + 1, (u + 1) % SLOTS)
                    blk = numbers_of(nc, ENG.DVE, V["blk_row"], g + 1, BLOCKS - 1)
                    for k in range(G):
                        v.wait_ge(agg_ready.h, agg_ready.at(g, k + 1))
                        v.wait_ge(acc_done.h, acc_done.at(g, k))
                        to = acc[:, bass.ds(blk[k], 1), 0:width].rearrange("p a w -> p (a w)")
                        v.tensor_tensor(to, to, ps[:, k % 8, 0:width], ALU.add).then_inc(acc_done.h, 1)
            v.wait_ge(acc_done.h, acc_done.at(GROUPS - 1))

        @block.tensor
        def _(te):
            te.wait_ge(cleared.h, cleared.at(0, start))
            with te.Fori(0, LOOPS) as i:
                for u in range(SLOTS):
                    g = i * SLOTS + u
                    te.wait_ge(gathered[u].h, gathered[u].at(i))
                    te.wait_ge(hot_ready.h, hot_ready.at(g))
                    if types is not None:
                        te.wait_ge(types_hot.h, types_hot.at(g))
                    for k in range(G):
                        te.wait_ge(acc_done.h, acc_done.at(g - 1, k + 1))
                        te.matmul(ps[:, k % 8, 0:width], hot[:, u, k, :], rows[:, u, k, 0:width], start=True, stop=True).then_inc(agg_ready.h, 1)
    cleared.base += start
    if types is not None:
        types_hot.phase_ended(GROUPS)
    hot_ready.phase_ended(GROUPS + 1)
    agg_ready.phase_ended(GROUPS)
    acc_done.phase_ended(GROUPS)
    V["idx_ready"].phase_ended(GROUPS + SLOTS)
    for c in gathered:
        c.phase_ended(LOOPS)


def gat_phase(nc, a, V, table, we):
    (ps, rows, acc, hot, turned, edge_t, score, score_raw, score_er, shift, weight, rst_sb, run, ref, carry, drop, dropc, openhot,
     scale, er_sb, er_parts, er_rest, md_all, off, ident, iota, iota_neg) = (V[n] for n in (
         "ps", "rows", "acc", "hot", "turned", "edge_t", "score", "score_raw", "score_er", "shift", "weight", "rst_sb", "run",
         "ref", "carry", "drop", "dropc", "openhot", "scale", "er_sb", "er_parts", "er_rest", "md_all", "off", "ident", "iota",
         "iota_neg"))
    cleared, gathered, resets, md_in, edge_in = (V[n] for n in ("cleared", "gathered", "resets", "md_in", "edge_in"))
    (hot_ready, agg_ready, acc_done, turned_a, turned_ready, er_ready, fe_ready, fe_added, er_summed, hot_a, off_hot, score_a, score_b,
     score_turned, scan_a, scan_b, drop_a, drop_ready, ref_turned, drop_mm, shifted, weight_ready, scale_ready, msg_ready,
     rescaled) = (V[n] for n in (
         "hot_ready", "agg_ready", "acc_done", "turned_a", "turned_ready", "er_ready", "fe_ready", "fe_added", "er_summed", "hot_a", "off_hot",
         "score_a", "score_b", "score_turned", "scan_a", "scan_b", "drop_a", "drop_ready", "ref_turned", "drop_mm",
         "shifted", "weight_ready", "scale_ready", "msg_ready", "rescaled"))
    BANK_SMALL, BANK_SCORE, BANKS_FE = 1, 2, (0, 6, 7)
    BANKS = ((4, 5), (4, 5)) if we is not None else ((4, 5), (6, 7))
    er_ps = ps[:, BANK_SMALL, 0:G * 3 * H]
    ref_ps = ps[:, BANK_SMALL, G * 3 * H:G * 4 * H]
    drop_ps = ps[:, BANK_SCORE, 0:H]
    score_ps = ps[0:H, BANK_SCORE:BANK_SCORE + 2, :].rearrange("h b e -> h (b e)")
    AHEAD = 3
    start = 7

    def heads(ap):
        return ap.rearrange("p (h d) -> p h d", h=H)

    with nc.Block() as block:
        block.gpsimd(gather_rows(nc, V, table, ROW, 1, 1))

        @block.sync
        def _(sp):
            def edges(g, u):
                tile = numbers_of(nc, ENG.SP, V["tile_row"], g, TILES)
                sp.wait_ge(fe_ready.h, fe_ready.at(g - SLOTS))
                settle(sp, V)
                for k in range(G):
                    sp.dma_start(edge_t[:, u, k, :], a["edge"][bass.ds(tile[k], 1), :, :].rearrange("a p n -> (a p) n")).then_inc(edge_in[u].h, 16)

            def group(g, u):
                sp.wait_ge(scan_b.h, scan_b.at(g - SLOTS))
                settle(sp, V)
                sp.wait_ge(turned_a.h, turned_a.at(g - SLOTS))
                settle(sp, V)
                sp.dma_start(md_all[:, u, :], V["md_dram"][bass.ds(g * GE, GE)].rearrange("(a e) -> a e", a=1).to_broadcast([P, GE])).then_inc(md_in[u].h, 16)
                sp.dma_start(rst_sb[:, u, :], V["rst_dram"][bass.ds(g * GE, GE + 1)].rearrange("(a e) -> a e", a=1).to_broadcast([H, GE + 1])).then_inc(resets[u].h, 16)
                if we is not None:
                    edges(g, u)

            with sp.Fori(0, LOOPS) as i:
                for u in range(SLOTS):
                    group(i * SLOTS + u, u)
            for g in (GROUPS, GROUPS + 1):
                sp.wait_ge(scan_b.h, scan_b.at(g - SLOTS))
                sp.wait_ge(turned_a.h, turned_a.at(g - SLOTS))
                settle(sp, V)
                sp.dma_start(md_all[:, g % SLOTS, :], V["md_dram"][g * GE:(g + 1) * GE].rearrange("(a e) -> a e", a=1).to_broadcast([P, GE])).then_inc(md_in[g % SLOTS].h, 16)
            if we is not None:
                edges(GROUPS, GROUPS % SLOTS)
            sp.wait_ge(turned_a.h, turned_a.at(GROUPS + 1))

        @block.vector
        def _(v):
            def add_edge_part(g, u, i, ks):
                v.wait_ge(gathered[u].h, gathered[u].at(i))
                for k in ks:
                    v.wait_ge(fe_ready.h, fe_ready.at(g, k + 1))
                    v.tensor_tensor(rows[:, u, k, :], rows[:, u, k, :], ps[:, BANKS_FE[(u * G + k) % 3], 0:ROW], ALU.add).then_inc(fe_added.h, 1)

            def sum_er(g):
                v.wait_ge(er_ready.h, er_ready.at(g))
                v.tensor_reduce(score_er[:, :, :], er_ps.rearrange("p (g t h) -> p g h t", g=G, t=3), mybir.AxisListType.X, ALU.add).then_inc(er_summed.h, 1)

            def scores(g, u, i):
                v.wait_ge(gathered[u].h, gathered[u].at(i))
                v.wait_ge(er_summed.h, er_summed.at(g))
                if we is not None:
                    v.wait_ge(fe_added.h, fe_added.at(g))
                v.tensor_tensor(score_raw[:, u, :, :], rows[:, u, :, FW:ROW], score_er[:, :, :], ALU.add).then_inc(score_a.h, 1)
                v.wait_ge(score_a.h, score_a.at(g))
                v.scalar_tensor_tensor(out=score[:, u, :, :], in0=score_raw[:, u, :, :], scalar=SLOPE, in1=score_raw[:, u, :, :], op0=ALU.mult, op1=ALU.max).then_inc(score_b.h, 1)

            def add_sums(unit, rec, n):
                ks = range(n * HALF, (n + 1) * HALF)

                def add(block, bank, gain):
                    to = acc[:, bass.ds(block, 1), 0:FW].rearrange("p a w -> p (a w)")
                    v.tensor_tensor(to, to, ps[:, bank, 0:FW], ALU.add).then_inc(acc_done.h, gain)

                with v.If(rec[2 + n] < FARTHER):
                    v.wait_ge(agg_ready.h, agg_ready.at(unit, ks[-1] + 1))
                    v.wait_ge(acc_done.h, acc_done.at(unit, ks[0]))
                    settle(v, V)
                    with v.If(rec[2 + n] == 0):
                        add(rec[n], BANKS[n][0], HALF)
                    with v.Else():
                        add(rec[n], BANKS[n][0], HALF - 1)
                        add(rec[5 + n], BANKS[n][1], 1)
                with v.Else():
                    blk = numbers_of(nc, ENG.DVE, V["blk_row"], unit, BLOCKS - 1)
                    for k in ks:
                        v.wait_ge(agg_ready.h, agg_ready.at(unit, k + 1))
                        v.wait_ge(acc_done.h, acc_done.at(unit, k))
                        add(blk[k], BANKS[n][k % len(BANKS[n])], 1)

            v.memset(acc[:, :, :], 0.0)
            v.memset(hot[:, SLOTS - 1, :, :], 0.0)
            v.memset(rows[:, SLOTS - 1, :, :], 0.0)
            v.memset(carry[:, :], -BIG).then_inc(cleared.h, 1)
            v.tensor_copy(er_parts[:, :, 0, :], er_sb[:, :, :]).then_inc(cleared.h, 1)
            v.wait_ge(cleared.h, cleared.at(0, 2))
            v.tensor_tensor(er_rest[:, :, :], er_sb[:, :, :], er_parts[:, :, 0, :], ALU.subtract).then_inc(cleared.h, 1)
            v.wait_ge(cleared.h, cleared.at(0, 3))
            v.tensor_copy(er_parts[:, :, 1, :], er_rest[:, :, :]).then_inc(cleared.h, 1)
            v.wait_ge(cleared.h, cleared.at(0, 4))
            v.tensor_tensor(er_rest[:, :, :], er_rest[:, :, :], er_parts[:, :, 1, :], ALU.subtract).then_inc(cleared.h, 1)
            v.wait_ge(cleared.h, cleared.at(0, 5))
            v.tensor_copy(er_parts[:, :, 2, :], er_rest[:, :, :]).then_inc(cleared.h, 1)
            v.engine_nop().then_inc(msg_ready.h, 2)
            v.engine_nop().then_inc(hot_ready.h, 1)
            v.engine_nop().then_inc(cleared.h, 1)
            if we is not None:
                add_edge_part(0, 0, 0, range(G))
            sum_er(0)
            scores(0, 0, 0)
            with v.Fori(0, LOOPS) as i:
                for u in range(SLOTS):
                    g, prev, nxt = i * SLOTS + u, (u - 1) % SLOTS, (u + 1) % SLOTS
                    nxt_i = i + 1 if nxt == 0 else i
                    v.wait_ge(resets[u].h, resets[u].at(i))
                    v.wait_ge(score_turned.h, score_turned.at(g))
                    v.tensor_tensor_scan(run[:, :], rst_sb[:, u, 0:GE], score_ps, carry[:, prev:prev + 1], ALU.add, ALU.max).then_inc(scan_a.h, 1)
                    v.tensor_scalar(openhot[:, u, :], iota[0:H, :], V["open_md"][:, bass.ds(g, 1)], None, ALU.is_equal)
                    v.wait_ge(scan_a.h, scan_a.at(g))
                    v.wait_ge(ref_turned.h, ref_turned.at(g - 1))
                    v.tensor_tensor_scan(ref[:, ::-1], rst_sb[:, u, GE:0:-1], run[:, ::-1], -BIG, ALU.add, ALU.max).then_inc(scan_b.h, 1)
                    v.tensor_copy(carry[:, u:u + 1], run[:, GE - 1:GE]).then_inc(drop_a.h, 1)
                    rec = numbers_at(nc, ENG.DVE, V["record"][0:1, bass.ds(g, 1), :], BLOCKS - 1)
                    v.wait_ge(scan_b.h, scan_b.at(g))
                    v.tensor_tensor(dropc[:, u:u + 1], carry[:, prev:prev + 1], ref[:, 0:1], ALU.subtract).then_inc(drop_a.h, 1)
                    v.wait_ge(drop_a.h, drop_a.at(g))
                    v.tensor_scalar(drop[:, u, :], ident[0:H, 0:H], dropc[:, u:u + 1], None, ALU.mult).then_inc(drop_ready.h, 1)
                    if we is None:
                        add_sums(g, rec, 0)
                    v.wait_ge(ref_turned.h, ref_turned.at(g))
                    v.tensor_tensor(shift[:, u, :, :], score[:, u, :, :], ref_ps.rearrange("p (g h) -> p g h", g=G), ALU.subtract).then_inc(shifted.h, 1)
                    if we is None:
                        sum_er(g + 1)
                    else:
                        add_edge_part(g + 1, nxt, nxt_i, range(AHEAD))
                    v.wait_ge(weight_ready.h, weight_ready.at(g))
                    for n in range(2):
                        part = rows[:, u, n * HALF:(n + 1) * HALF, 0:FW].rearrange("p g (h d) -> p g h d", h=H)
                        v.tensor_tensor(part, part, weight[:, u, n * HALF:(n + 1) * HALF, :].unsqueeze(3).to_broadcast([P, HALF, H, HW]), ALU.mult).then_inc(msg_ready.h, 1)
                        if we is not None and n == 0:
                            add_edge_part(g + 1, nxt, nxt_i, range(AHEAD, AHEAD + 2))
                    if we is not None:
                        add_sums(g, rec, 0)
                        add_edge_part(g + 1, nxt, nxt_i, range(AHEAD + 2, G))
                        sum_er(g + 1)
                    scores(g + 1, nxt, nxt_i)
                    add_sums(g, rec, 1)
                    v.wait_ge(scale_ready.h, scale_ready.at(g))
                    v.wait_ge(acc_done.h, acc_done.at(g))
                    to = heads(acc[:, bass.ds(rec[4], 1), 0:FW].rearrange("p a w -> p (a w)"))
                    v.tensor_tensor(to, to, scale[:, u, :].unsqueeze(2).to_broadcast([P, H, HW]), ALU.mult).then_inc(rescaled.h, 1)
                    v.wait_ge(rescaled.h, rescaled.at(g))
            rec = numbers_at(nc, ENG.DVE, V["record"][0:1, GROUPS:GROUPS + 1, :], BLOCKS - 1)
            for n in range(2):
                add_sums(GROUPS, rec, n)
            v.wait_ge(acc_done.h, acc_done.at(GROUPS))

        @block.tensor
        def _(te):
            def er_of(g, u):
                blk = numbers_of(nc, ENG.PE, V["blk_row"], g + 1, BLOCKS - 1)
                te.wait_ge(er_summed.h, er_summed.at(g - 1))
                te.wait_ge(shifted.h, shifted.at(g - 2 if we is None else g - 1))
                te.wait_ge(turned_ready.h, turned_ready.at(g))
                for k in range(G):
                    mm = te.matmul(er_ps[:, k * 3 * H:(k + 1) * 3 * H], turned[:, k * P:(k + 1) * P],
                                   er_parts[:, :, :, :].rearrange("p b t h -> p (b t h)")[:, bass.ds(blk[k] * (3 * H), 3 * H)], start=True, stop=True)
                mm.then_inc(er_ready.h, 1)

            def project_edges(g, u, i, ks):
                te.wait_ge(edge_in[u].h, edge_in[u].at(i))
                for k in ks:
                    te.wait_ge(fe_added.h, fe_added.at(g, k - 2))
                    for c in range(2):
                        mm = te.matmul(ps[:, BANKS_FE[(u * G + k) % 3], 0:ROW], edge_t[:, u, k, c * P:(c + 1) * P], we[:, c, 0:ROW], start=(c == 0), stop=(c == 1))
                    mm.then_inc(fe_ready.h, 1)

            def turn_scores(g, u):
                te.wait_ge(score_b.h, score_b.at(g))
                te.wait_ge(scan_a.h, scan_a.at(g - 1))
                te.wait_ge(scale_ready.h, scale_ready.at(g - 1))
                settle(te, V)
                for k in range(G):
                    mm = te.transpose(score_ps[:, k * P:(k + 1) * P], score[:, u, k, :], ident[:, :])
                mm.then_inc(score_turned.h, 1)

            def sums(unit, u, rec, n):
                ks = range(n * HALF, (n + 1) * HALF)
                te.wait_ge(msg_ready.h, msg_ready.at(unit, n + 1))
                te.wait_ge(hot_ready.h, hot_ready.at(unit))
                if we is None:
                    te.wait_ge(acc_done.h, acc_done.at(unit - 1, ks[-1] + 1))
                else:
                    te.wait_ge(acc_done.h, acc_done.at(unit, ks[0]))
                settle(te, V)

                def several_turns():
                    for k in ks:
                        if k - ks[0] >= len(BANKS[n]):
                            te.wait_ge(acc_done.h, acc_done.at(unit, k - len(BANKS[n]) + 1))
                        te.matmul(ps[:, BANKS[n][k % len(BANKS[n])], 0:FW], hot[:, u, k, :], rows[:, u, k, 0:FW], start=True, stop=True).then_inc(agg_ready.h, 1)

                def block_sums(bank, part):
                    for k in part:
                        mm = te.matmul(ps[:, bank, 0:FW], hot[:, u, k, :], rows[:, u, k, 0:FW], start=(k == part[0]), stop=(k == part[-1]))
                    mm.then_inc(agg_ready.h, len(part))

                def one_turn(t):
                    if t == HALF:
                        return several_turns()
                    with te.If(rec[2 + n] == ONE_TURN[t]):
                        block_sums(BANKS[n][0], ks[:t])
                        block_sums(BANKS[n][1], ks[t:])
                    with te.Else():
                        one_turn(t + 1)

                with te.If(rec[2 + n] == 0):
                    block_sums(BANKS[n][0], ks)
                with te.Else():
                    one_turn(1)

            te.wait_ge(cleared.h, cleared.at(0, start))
            er_of(0, 0)
            if we is not None:
                project_edges(0, 0, 0, range(G))
            turn_scores(0, 0)
            with te.Fori(0, LOOPS) as i:
                for u in range(SLOTS):
                    g, prev, nxt = i * SLOTS + u, (u - 1) % SLOTS, (u + 1) % SLOTS
                    rec = numbers_at(nc, ENG.PE, V["record"][0:1, bass.ds(g, 1), :], BLOCKS - 1)
                    if we is not None:
                        project_edges(g + 1, nxt, i + 1 if nxt == 0 else i, range(AHEAD))
                    sums(g, prev, rec, 0)
                    if we is None:
                        er_of(g + 1, nxt)
                    te.wait_ge(scan_b.h, scan_b.at(g))
                    te.wait_ge(shifted.h, shifted.at(g - 1))
                    te.wait_ge(er_summed.h, er_summed.at(g))
                    settle(te, V)
                    for k in range(G):
                        mm = te.transpose(ref_ps[:, k * H:(k + 1) * H], ref[:, k * P:(k + 1) * P], ident[0:H, 0:H])
                    mm.then_inc(ref_turned.h, 1)
                    te.wait_ge(drop_ready.h, drop_ready.at(g))
                    te.matmul(drop_ps, openhot[:, u, :], drop[:, u, :], start=True, stop=True).then_inc(drop_mm.h, 1)
                    if we is not None:
                        project_edges(g + 1, nxt, i + 1 if nxt == 0 else i, range(AHEAD, G))
                        er_of(g + 1, nxt)
                    sums(g, prev, rec, 1)
                    turn_scores(g + 1, nxt)
            rec = numbers_at(nc, ENG.PE, V["record"][0:1, GROUPS:GROUPS + 1, :], BLOCKS - 1)
            for n in range(2):
                sums(GROUPS, (GROUPS - 1) % SLOTS, rec, n)

        @block.scalar
        def _(act):
            def turned_hot(g, u, i):
                act.wait_ge(md_in[u].h, md_in[u].at(i))
                act.wait_ge(turned_ready.h, turned_ready.at(g - 1))
                act.activation(off[:, :], md_all[:, u, :], ACT.Abs, bias=iota_neg[:, 0:1]).then_inc(turned_a.h, 1)
                act.wait_ge(er_ready.h, er_ready.at(g - 1))
                act.wait_ge(turned_a.h, turned_a.at(g))
                act.activation(turned[:, :], off[:, :], ACT.Relu, bias=1.0, scale=-1.0).then_inc(turned_ready.h, 1)

            def straight_hot(g, u):
                act.wait_ge(hot_ready.h, hot_ready.at(g))
                for k in range(G):
                    op = act.activation(off_hot[:, k, :], iota[:, :], ACT.Abs, bias=V["md_t"][:, bass.ds(g * G + k, 1)], scale=-1.0)
                op.then_inc(hot_a.h, 1)
                act.wait_ge(agg_ready.h, agg_ready.at(g + 1 - SLOTS))
                act.wait_ge(hot_a.h, hot_a.at(g))
                act.activation(hot[:, u, :, :], off_hot[:, :, :], ACT.Relu, bias=1.0, scale=-1.0).then_inc(hot_ready.h, 1)

            for u in range(SLOTS):
                give_sources(act, V, u, u)
            straight_hot(0, 0)
            turned_hot(0, 0, 0)
            turned_hot(1, 1, 0)
            with act.Fori(0, LOOPS) as i:
                for u in range(SLOTS):
                    g, ahead = i * SLOTS + u, (u + 2) % SLOTS
                    act.wait_ge(drop_mm.h, drop_mm.at(g))
                    act.activation(scale[:, u, :], drop_ps, ACT.Exp).then_inc(scale_ready.h, 1)
                    act.wait_ge(shifted.h, shifted.at(g))
                    act.activation(weight[:, u, :, :], shift[:, u, :, :], ACT.Exp).then_inc(weight_ready.h, 1)
                    give_sources(act, V, g + SLOTS, u, i)
                    turned_hot(g + 2, ahead, i + 1 if ahead < 2 else i)
                    straight_hot(g + 1, (u + 1) % SLOTS)

    cleared.base += start
    for c in (hot_a, er_ready, er_summed, score_a, score_b, score_turned, agg_ready, acc_done):
        c.phase_ended(GROUPS + 1)
    msg_ready.phase_ended(GROUPS + 1)
    V["idx_ready"].phase_ended(GROUPS + SLOTS)
    for c in (hot_ready, turned_a, turned_ready):
        c.phase_ended(GROUPS + 2)
    for c in (scan_a, scan_b, drop_a, drop_ready, ref_turned, drop_mm, shifted, weight_ready, scale_ready, rescaled):
        c.phase_ended(GROUPS)
    for u in range(SLOTS):
        more = 1 if u == GROUPS % SLOTS else 0
        gathered[u].phase_ended(LOOPS + more)
        resets[u].phase_ended(LOOPS)
        md_in[u].phase_ended(LOOPS + (1 if u in (GROUPS % SLOTS, (GROUPS + 1) % SLOTS) else 0))
        if we is not None:
            edge_in[u].phase_ended(LOOPS + more)
    if we is not None:
        fe_ready.phase_ended(GROUPS + 1)
        fe_added.phase_ended(GROUPS + 1)


def node_phase(nc, a, V, kind, x_dram, out_dram, table, w):
    ps, acc, ident, ones, er_sb = (V[n] for n in ("ps", "acc", "ident", "ones", "er_sb"))
    (x_in, c_turned, c_copied, turned_in, copied_in, products, gates, arg, tanh, used_in, x_new, turned_out, copied_out,
     table_mm, table_copied, dve_step, stored, store_x, store_t, red_copied, gru_a, norm_step, rstd) = (V[n] for n in (
         "x_in", "c_turned", "c_copied", "turned_in", "copied_in", "products", "gates", "arg", "tanh", "used_in",
         "x_new", "turned_out", "copied_out", "table_mm", "table_copied", "dve_step", "stored", "store_x", "store_t", "red_copied", "gru_a", "norm_step", "rstd"))
    flat = {n: V[n][:, :, :, :].rearrange("p a b c -> p (a b c)") for n in ("rows", "edge_t", "hot")}

    def part(buf, at, width):
        return flat[buf][:, at:at + BATCH * width].rearrange("p (i d) -> p i d", i=BATCH)

    tin = part("rows", 0, 2 * D)
    tab = part("rows", BATCH * 2 * D, ROW)
    y = part("edge_t", 0, D)
    pre = part("edge_t", BATCH * D, D)
    xin = part("edge_t", 2 * BATCH * D, D)
    zg = part("hot", 0, D)
    ct = part("hot", BATCH * D, P)
    rg = tin[:, :, D:2 * D]
    small = V["nsmall"]
    rec, stats, mv = small[:, :, 0:H], small[:, :, H:H + 6], small[:, :, H + 6:H + 8]
    project = kind in ("sage", "gru")
    norm = kind != "mid"
    need_x = x_dram is not None
    tdram, wt = table if table else (None, None)

    def heads(ap):
        return ap.rearrange("p (h d) -> p h d", h=H)

    with nc.Block() as block:
        @block.sync
        def _(sp):
            with sp.Fori(0, NBATCH) as i:
                if need_x:
                    sp.wait_ge(x_new.h, x_new.at(i * BATCH - 1))
                    settle(sp, V)
                    sp.dma_start(xin, x_dram[bass.ds(i * (BATCH * P), BATCH * P), :].rearrange("(b p) d -> p b d", p=P)).then_inc(x_in.h, 16)
                if out_dram is not None:
                    sp.wait_ge(x_new.h, x_new.at(i * BATCH + BATCH - 1))
                    settle(sp, V)
                    sp.dma_start(out_dram[bass.ds(i * (BATCH * P), BATCH * P), :].rearrange("(b p) d -> p b d", p=P), y).then_inc(store_x.h, 16)
                if table:
                    sp.wait_ge(table_copied.h, table_copied.at(i * BATCH + BATCH - 1))
                    settle(sp, V)
                    sp.dma_start(tdram[bass.ds(i * (BATCH * P), BATCH * P), :].rearrange("(b p) d -> p b d", p=P), tab).then_inc(store_t.h, 16)
                    sp.wait_ge(store_t.h, store_t.at(i))
                    settle(sp, V)
                if out_dram is not None:
                    sp.wait_ge(store_x.h, store_x.at(i))
                sp.sem_inc(stored.h, 1)

        @block.vector
        def _(v):
            if table:
                for j in range(BATCH):
                    op = v.memset(heads(tab[:, j, 0:FW])[:, :, HD:HW], 1.0)
                op.then_inc(V["cleared"].h, 1)
            with v.Fori(0, NBATCH) as i:
                step = [0]

                def block_of(j):
                    return bass.ds(i * BATCH + j, 1)

                def one(ap):
                    return ap.rearrange("p a w -> p (a w)")

                def ended(op):
                    op.then_inc(dve_step.h, 1)
                    step[0] += 1
                    v.wait_ge(dve_step.h, dve_step.at(i, step[0]))

                js = range(BATCH)
                v.wait_ge(x_new.h, x_new.at(i * BATCH - 1))
                if kind == "sage":
                    for j in js:
                        op = v.tensor_scalar(rec[:, j, 0:1], one(acc[:, block_of(j), D:D + 1]), 1.0, None, ALU.max)
                    ended(op)
                    for j in js:
                        op = v.reciprocal(rec[:, j, 0:1], rec[:, j, 0:1])
                    ended(op)
                    for j in js:
                        v.tensor_scalar(pre[:, j, :], one(acc[:, block_of(j), 0:D]), rec[:, j, 0:1], None, ALU.mult).then_inc(arg.h, 1)
                if kind in ("gat", "mid", "last"):
                    for j in js:
                        op = v.tensor_scalar(rec[:, j, :].unsqueeze(2), heads(one(acc[:, block_of(j), 0:FW]))[:, :, HD:HW], 0.5, None, ALU.max)
                    ended(op)
                    for j in js:
                        op = v.reciprocal(rec[:, j, :], rec[:, j, :])
                    ended(op)
                    for j in js:
                        op = v.tensor_tensor(heads(pre[:, j, :]), heads(one(acc[:, block_of(j), 0:FW]))[:, :, 0:HD],
                                             rec[:, j, :].unsqueeze(2).to_broadcast([P, H, HD]), ALU.mult)
                    ended(op)
                    bias = w[{"gat": "b2", "mid": "b3a", "last": "b3b"}[kind] + "_all"]
                    for j in js:
                        op = v.tensor_tensor(pre[:, j, :], pre[:, j, :], bias[:, :], ALU.add)
                    if kind == "gat":
                        ended(op)
                        v.wait_ge(x_in.h, x_in.at(i))
                        op = v.tensor_tensor(pre, pre, xin, ALU.add)
                    ended(op)
                if kind == "gru":
                    for j in js:
                        v.tensor_copy(small[:, j, 0:NREL], one(acc[:, block_of(j), D:D + NREL]))
                        v.tensor_copy(pre[:, j, :], one(acc[:, block_of(j), 0:D])).then_inc(red_copied.h, 1)
                    for j in js:
                        v.wait_ge(gates.h, gates.at(i * BATCH + j))
                        v.tensor_tensor(pre[:, j, :], rg[:, j, :], ps[:, 5 + j % 2, D:2 * D], ALU.mult).then_inc(gru_a.h, 1)
                        v.wait_ge(gru_a.h, gru_a.at(i * BATCH + j))
                        v.tensor_tensor(pre[:, j, :], pre[:, j, :], ps[:, 5 + j % 2, 0:D], ALU.add).then_inc(arg.h, 1)
                    v.wait_ge(tanh.h, tanh.at(i * BATCH + BATCH - 1))
                    v.wait_ge(x_in.h, x_in.at(i))
                    ended(v.tensor_tensor(rg, xin, pre, ALU.subtract))
                    ended(v.tensor_tensor(rg, rg, zg, ALU.mult))
                    ended(v.tensor_tensor(rg, rg, pre, ALU.add))
                v.wait_ge(stored.h, stored.at(i - 1))
                if kind == "sage":
                    v.wait_ge(x_in.h, x_in.at(i))
                    for j in js:
                        v.wait_ge(products.h, products.at(i * BATCH + j))
                        op = v.tensor_tensor(y[:, j, :], ps[:, 3 + j % 2, 0:D], xin[:, j, :], ALU.add)
                        op.then_inc(used_in.h, 1)
                    v.wait_ge(used_in.h, used_in.at(i * BATCH + BATCH - 1))
                elif kind == "gru":
                    ended(v.tensor_tensor(y, rg, xin, ALU.add))
                elif kind == "mid":
                    for j in js:
                        v.tensor_scalar(y[:, j, :], pre[:, j, :], 0.0, None, ALU.max).then_inc(x_new.h, 1)
                else:
                    if kind == "last":
                        v.wait_ge(x_in.h, x_in.at(i))
                    ended(v.scalar_tensor_tensor(out=y, in0=pre, scalar=0.0, in1=xin, op0=ALU.max, op1=ALU.add))
                if norm:
                    for j in js:
                        op = v.bn_stats(stats[:, j, :], y[:, j, :])
                    op.then_inc(norm_step.h, 1)
                    v.wait_ge(norm_step.h, norm_step.at(i, 1))
                    settle(v, V)
                    for j in js:
                        op = v.bn_aggr(mv[:, j, :], stats[:, j, :])
                    op.then_inc(norm_step.h, 1)
                    v.wait_ge(norm_step.h, norm_step.at(i, 2))
                    v.tensor_scalar(mv[:, :, 1:2], mv[:, :, 1:2], EPS, None, ALU.add).then_inc(norm_step.h, 1)
                    v.wait_ge(rstd.h, rstd.at(i))
                    v.reciprocal(mv[:, :, 1:2], mv[:, :, 1:2]).then_inc(norm_step.h, 1)
                    v.wait_ge(norm_step.h, norm_step.at(i, 4))
                    for j in js:
                        v.tensor_scalar(y[:, j, :], y[:, j, :], mv[:, j, 0:1], mv[:, j, 1:2], ALU.subtract, ALU.mult).then_inc(x_new.h, 1)
                v.engine_nop().then_inc(dve_step.h, 8 - step[0])

        @block.scalar
        def _(act):
            with act.Fori(0, NBATCH) as i:
                js = range(BATCH)
                if kind == "gru":
                    for j in js:
                        act.wait_ge(c_turned.h, c_turned.at(i * BATCH + j))
                        act.copy(ct[0:NREL, j, :], ps[0:NREL, (2, 7)[j % 2], 0:P]).then_inc(c_copied.h, 1)
                if project:
                    for j in js:
                        act.wait_ge(turned_in.h, turned_in.at(i * BATCH + j))
                        act.copy(tin[:, j, :], ps[:, j % 2, :]).then_inc(copied_in.h, 1)
                if kind == "gru":
                    for j in js:
                        act.wait_ge(products.h, products.at(i * BATCH + j))
                        act.activation(rg[:, j, :], ps[:, 3 + j % 2, 0:D], ACT.Sigmoid)
                        act.activation(zg[:, j, :], ps[:, 3 + j % 2, D:2 * D], ACT.Sigmoid).then_inc(gates.h, 1)
                    act.wait_ge(arg.h, arg.at(i * BATCH + BATCH - 1))
                    for j in js:
                        act.activation(pre[:, j, :], pre[:, j, :], ACT.Tanh).then_inc(tanh.h, 1)
                if norm:
                    act.wait_ge(norm_step.h, norm_step.at(i, 3))
                    act.activation(mv[:, :, 1:2], mv[:, :, 1:2], ACT.Sqrt).then_inc(rstd.h, 1)
                if table:
                    for j in js:
                        act.wait_ge(turned_out.h, turned_out.at(i * BATCH + j))
                        act.copy(tin[:, j, 0:D], ps[:, j % 2, 0:D]).then_inc(copied_out.h, 1)
                    act.wait_ge(stored.h, stored.at(i - 1))
                    act.wait_ge(V["cleared"].h, V["cleared"].at(0, 1))
                    for j in js:
                        act.wait_ge(table_mm.h, table_mm.at(i * BATCH + j))
                        got = ps[:, 3 + j % 2, :]
                        act.copy(heads(tab[:, j, 0:FW])[:, :, 0:HD], heads(got[:, 0:FW])[:, :, 0:HD])
                        act.copy(tab[:, j, FW:ROW], got[:, FW:ROW])
                        act.copy(er_sb[:, bass.ds(i * BATCH + j, 1), :].rearrange("p a h -> p (a h)"), got[:, ROW:ROW + H]).then_inc(table_copied.h, 1)

        @block.tensor
        def _(te):
            with te.Fori(0, NBATCH) as i:
                js = range(BATCH)

                if kind == "gru":
                    te.wait_ge(c_copied.h, c_copied.at(i * BATCH - 1))
                    for j in js:
                        if j >= 2:
                            te.wait_ge(c_copied.h, c_copied.at(i * BATCH + j - 2))
                        te.wait_ge(red_copied.h, red_copied.at(i * BATCH + j))
                        te.transpose(ps[0:NREL, (2, 7)[j % 2], 0:P], small[:, j, 0:NREL], ident[:, :]).then_inc(c_turned.h, 1)
                if project:
                    te.wait_ge(x_in.h, x_in.at(i))
                    last = copied_out if table else copied_in
                    te.wait_ge(last.h, last.at(i * BATCH - 1))
                    for j in js:
                        if j >= 2:
                            te.wait_ge(copied_in.h, copied_in.at(i * BATCH + j - 2))
                        if kind == "sage":
                            te.wait_ge(arg.h, arg.at(i * BATCH + j))
                        else:
                            te.wait_ge(c_copied.h, c_copied.at(i * BATCH + j))
                        for c in range(2):
                            to = ps[:, j % 2, c * P:(c + 1) * P]
                            if kind == "sage":
                                te.transpose(to, pre[:, j, c * P:(c + 1) * P], ident[:, :])
                            else:
                                te.matmul(to, pre[:, j, c * P:(c + 1) * P], ident[:, :], start=True, stop=False)
                                te.matmul(to, w["rel"][:, c * P:(c + 1) * P], ct[0:NREL, j, :], start=False, stop=True)
                        for c in range(2):
                            mm = te.transpose(ps[:, j % 2, (2 + c) * P:(3 + c) * P], xin[:, j, c * P:(c + 1) * P], ident[:, :])
                        mm.then_inc(turned_in.h, 1)
                    if table:
                        te.wait_ge(table_copied.h, table_copied.at(i * BATCH - 1))
                    for j in js:
                        te.wait_ge(copied_in.h, copied_in.at(i * BATCH + j))
                        n = i * BATCH + j
                        if kind == "sage":
                            te.wait_ge(used_in.h, used_in.at(n - 2))
                            for c in range(2):
                                te.matmul(ps[:, 3 + j % 2, 0:D], tin[:, j, c * P:(c + 1) * P], w["wn"][:, c, :], start=(c == 0), stop=False)
                            for c in range(2):
                                te.matmul(ps[:, 3 + j % 2, 0:D], tin[:, j, (2 + c) * P:(3 + c) * P], w["ws"][:, c, :], start=False, stop=False)
                            te.matmul(ps[:, 3 + j % 2, 0:D], ones[0:1, :], w["b0"][:, :], start=False, stop=True).then_inc(products.h, 1)
                        else:
                            te.wait_ge(gates.h, gates.at(n - 2))
                            te.wait_ge(arg.h, arg.at(n - 2))
                            rz, hn, inn = ps[:, 3 + j % 2, :], ps[:, 5 + j % 2, D:2 * D], ps[:, 5 + j % 2, 0:D]
                            for c in range(2):
                                te.matmul(rz, tin[:, j, c * P:(c + 1) * P], w["wih"][:, c, 0:2 * D], start=(c == 0), stop=False)
                            for c in range(2):
                                te.matmul(rz, tin[:, j, (2 + c) * P:(3 + c) * P], w["whh"][:, c, 0:2 * D], start=False, stop=False)
                            te.matmul(rz, ones[0:1, :], w["brz"][:, :], start=False, stop=True)
                            for to, at, ww, b in ((inn, 0, w["wih"], w["bih"]), (hn, 2, w["whh"], w["bhh"])):
                                for c in range(2):
                                    te.matmul(to, tin[:, j, (at + c) * P:(at + c + 1) * P], ww[:, c, 2 * D:], start=(c == 0), stop=False)
                                mm = te.matmul(to, ones[0:1, :], b[:, 2 * D:], start=False, stop=True)
                            mm.then_inc(products.h, 1)
                if table:
                    if project:
                        te.wait_ge(copied_in.h, copied_in.at(i * BATCH + BATCH - 1))
                    for j in js:
                        te.wait_ge(x_new.h, x_new.at(i * BATCH + j))
                        te.wait_ge(copied_out.h, copied_out.at(i * BATCH + j - 2))
                        for c in range(2):
                            mm = te.transpose(ps[:, j % 2, c * P:(c + 1) * P], y[:, j, c * P:(c + 1) * P], ident[:, :])
                        mm.then_inc(turned_out.h, 1)
                    if kind == "gru":
                        te.wait_ge(gates.h, gates.at(i * BATCH + BATCH - 1))
                    for j in js:
                        te.wait_ge(copied_out.h, copied_out.at(i * BATCH + j))
                        te.wait_ge(table_copied.h, table_copied.at(i * BATCH + j - 2))
                        for c in range(2):
                            mm = te.matmul(ps[:, 3 + j % 2, 0:FW + 2 * H], tin[:, j, c * P:(c + 1) * P], wt[:, c, :], start=(c == 0), stop=(c == 1))
                        mm.then_inc(table_mm.h, 1)

    dve_step.phase_ended(NBATCH)
    stored.phase_ended(NBATCH)
    if need_x:
        x_in.phase_ended(NBATCH)
    if out_dram is not None:
        store_x.phase_ended(NBATCH)
    x_new.phase_ended(BLOCKS)
    if norm:
        norm_step.phase_ended(NBATCH)
        rstd.phase_ended(NBATCH)
    if project:
        for c in (turned_in, copied_in, products, arg):
            c.phase_ended(BLOCKS)
        if kind == "sage":
            used_in.phase_ended(BLOCKS)
    if kind == "gru":
        for c in (c_turned, c_copied, gates, tanh, gru_a, red_copied):
            c.phase_ended(BLOCKS)
    if table:
        V["cleared"].base += 1
        store_t.phase_ended(NBATCH)
        for c in (turned_out, copied_out, table_mm, table_copied):
            c.phase_ended(BLOCKS)


_OUT_ROWS = NPAD


def kernel(**inputs):
    import numpy as np
    import concourse.bacc as bacc
    from concourse.bass_utils import run_bass_kernel_spmd as launch

    def arr(name):
        return np.ascontiguousarray(inputs[name])

    def padded(x, rows, fill):
        out = np.full((rows,) + x.shape[1:], fill, x.dtype)
        out[:x.shape[0]] = x
        return out

    edges = TROWS * P
    dst = padded(arr("dst"), edges, NPAD)
    feat = {"x": padded(arr("x"), NPAD, 0),
            "src": padded(arr("src"), edges, 0).reshape(TROWS, P),
            "dst": dst.reshape(TROWS, P),
            "etype": padded(arr("edge_type_16"), edges, 0).reshape(TROWS, P),
            "dlast": np.ascontiguousarray(dst[P - 1:TILES * P:P]),
            "edge": np.ascontiguousarray(padded(arr("edge_attr_256"), edges, 0).reshape(TROWS, P, 2, P).transpose(0, 3, 2, 1)).reshape(TROWS, P, D)}
    feat["ws"], feat["wn"], feat["b0"] = arr("L0_gnn_W_self"), arr("L0_gnn_W_neigh"), arr("L0_gnn_b")
    feat["rel"], feat["bih"], feat["bhh"] = arr("L1_gnn_relvectors"), arr("L1_gnn_b_ih"), arr("L1_gnn_b_hh")
    feat["wih"], feat["whh"] = (np.ascontiguousarray(arr(n).T) for n in ("L1_gnn_w_ih", "L1_gnn_w_hh"))
    for name, x in (("w2", arr("L2_gnn_W").T), ("we", arr("L2_gnn_We").T), ("w3a", arr("L3_gnn_W1")), ("w3b", arr("L3_gnn_W2"))):
        feat[name], feat[name + "_t"] = np.ascontiguousarray(x), np.ascontiguousarray(x.T)
    for name, x in (("al2", "L2_gnn_attn_l"), ("ar2", "L2_gnn_attn_r"), ("ae2", "L2_gnn_attn_e"), ("al3a", "L3_gnn_al1"),
                    ("ar3a", "L3_gnn_ar1"), ("al3b", "L3_gnn_al2"), ("ar3b", "L3_gnn_ar2")):
        feat[name] = arr(x).reshape(-1)
    feat["bias2"], feat["bias3a"], feat["bias3b"] = arr("L2_gnn_bias"), arr("L3_gnn_b1"), arr("L3_gnn_b2")
    feat["b2"], feat["b3a"], feat["b3b"] = feat.pop("bias2"), feat.pop("bias3a"), feat.pop("bias3b")
    feat["ident"] = np.eye(P, dtype=np.float32)
    feat["kio"] = np.arange(KPAD, dtype=np.float32)
    feat["kcol"] = np.ascontiguousarray(np.arange(KPAD, dtype=np.float32).reshape(CHUNKS, P).T)
    feat["pcol"] = np.arange(P, dtype=np.float32).reshape(P, 1)
    feat["headmask"] = np.kron(np.eye(H, dtype=np.float32), np.ones((HD, 1), np.float32))

    nc = bacc.Bacc("TRN2", target_bir_lowering=False, num_devices=1)
    aps, sent = {}, {}
    for name, x in feat.items():
        sent[f"in_{name}"] = x
        aps[name] = nc.dram_tensor(f"in_{name}", x.shape, mybir.dt.from_np(x.dtype), kind="ExternalInput").ap()
    aps["out"] = nc.dram_tensor("out_0", (NPAD, D), F32, kind="ExternalOutput").ap()
    build(nc, aps)
    r = launch(nc, [sent], core_ids=[0])
    return r.results[0]["out_0"][:N]
```
